# Optimizing a Trainium2 kernel written in Bass

```python
import numpy as np
import jax
import jax.numpy as jnp

def _softmax(x, axis=-1):
    return jax.nn.softmax(x, axis=axis)

def _gelu(x):
    return jax.nn.gelu(x, approximate=True)

def _silu(x):
    return jax.nn.silu(x)

def _sigmoid(x):
    return jax.nn.sigmoid(x)

def _layernorm(x, axis=-1, eps=1e-05):
    m = jnp.mean(x, axis=axis, keepdims=True)
    v = jnp.var(x, axis=axis, keepdims=True)
    return (x - m) / jnp.sqrt(v + eps)

def _scatter_add(tgt, idx, src, axis=0):
    return tgt.at[idx].add(src)

def _segment_sum(src, seg, n):
    return jax.ops.segment_sum(src, seg, n)
kernel_name = 'mk_xattn_ffn_d1_seqx_r8_42361f'

def setup_inputs(seed: int=0):
    np.random.seed(seed)
    _w = jnp.asarray

    def _rec_inputs():
        import jax
        import jax.numpy as jnp
        _rk = jax.random.key(seed)
        x = 7.22e-05 + 1 * jax.random.normal(jax.random.fold_in(_rk, 1), (2, 512, 128), jnp.float32)
        _lenS = 512 - jax.random.randint(jax.random.fold_in(_rk, 7), (2,), 0, max(1, 512 // 4) + 1, jnp.int32)
        _lenS2 = 32 - jax.random.randint(jax.random.fold_in(_rk, 8), (2,), 0, max(1, 32 // 4) + 1, jnp.int32)
        _ctx_1024P = jax.random.normal(jax.random.fold_in(_rk, 11), (2, 16, 128), jnp.float32)
        _ctx_1024c = jax.random.dirichlet(jax.random.fold_in(_rk, 511), 0.3 * jnp.ones((16,), jnp.float32), (2, 32))
        _ctx_1024t = jnp.einsum('bsk,bkd->bsd', _ctx_1024c, _ctx_1024P)
        _ctx_1024t = _ctx_1024t * jax.lax.rsqrt(jnp.mean(jnp.square(_ctx_1024t)) + 1e-12) * 0.953939
        ctx_1024 = 4.13588e-05 + 0.999923 * (_ctx_1024t + 0.3 * jax.random.normal(jax.random.fold_in(_rk, 611), (2, 32, 128), jnp.float32))
        _validS = jnp.arange(512)[None, :] < _lenS[:, None]
        _validS2 = jnp.arange(32)[None, :] < _lenS2[:, None]
        _causal = jnp.tril(jnp.ones((512, 512), dtype=bool))
        mask_BxS2_ik0 = jnp.where(jnp.broadcast_to(_validS2[:, :], (2, 32)), 0, 1).astype(jnp.int32)
        return (x, ctx_1024, mask_BxS2_ik0)
    x, ctx_1024, mask_BxS2_ik0 = _rec_inputs()

    def _L0_xattn_setup():
        import jax, jax.numpy as jnp
        import numpy as np
        EMB_DIM = 128
        NUM_HEADS = 16
        HEAD_DIM = EMB_DIM // NUM_HEADS
        B, S_Q, S_KV = (4, 256, 256)
        key = jax.random.key(seed)
        ks = jax.random.split(key, 12)
        s = EMB_DIM ** (-0.5)
        inp = {'q': jax.random.normal(ks[0], (B, S_Q, EMB_DIM), jnp.float32), 'k': jax.random.normal(ks[1], (B, S_KV, EMB_DIM), jnp.float32), 'v': jax.random.normal(ks[2], (B, S_KV, EMB_DIM), jnp.float32), 'mask': jax.random.randint(ks[3], (B, S_KV), 0, 2, jnp.int32), 'Wq': jax.random.normal(ks[4], (EMB_DIM, EMB_DIM), jnp.float32) * s, 'bq': jnp.zeros((EMB_DIM,), jnp.float32), 'Wk': jax.random.normal(ks[5], (EMB_DIM, EMB_DIM), jnp.float32) * s, 'bk': jnp.zeros((EMB_DIM,), jnp.float32), 'Wv': jax.random.normal(ks[6], (EMB_DIM, EMB_DIM), jnp.float32) * s, 'bv': jnp.zeros((EMB_DIM,), jnp.float32), 'Wo': jax.random.normal(ks[7], (EMB_DIM, EMB_DIM), jnp.float32) * s, 'bo': jnp.zeros((EMB_DIM,), jnp.float32)}
        return inp
    _L0_xattn_all = _L0_xattn_setup()
    _L0_xattn_in = {k: v for k, v in _L0_xattn_all.items() if k in ('Wq', 'bq', 'Wk', 'bk', 'Wv', 'bv', 'Wo', 'bo')}
    del _L0_xattn_all

    def _L0_ffn_setup():
        import jax, jax.numpy as jnp
        import numpy as np
        D_MODEL = 128
        D_FF = 512
        N_EXPERTS = 8
        TOP_K = 2

        def _ffn(x, w1, b1, w2, b2):
            h = jax.nn.gelu(x @ w1.T + b1)
            return h @ w2.T + b2
        key = jax.random.key(seed)
        ks = jax.random.split(key, 12)
        s = 0.02
        x = jax.random.normal(ks[0], (4, 256, D_MODEL), dtype=jnp.float32)
        shared_w1 = jax.random.normal(ks[1], (D_FF, D_MODEL), dtype=jnp.float32) * s
        shared_b1 = jnp.zeros((D_FF,), dtype=jnp.float32)
        shared_w2 = jax.random.normal(ks[2], (D_MODEL, D_FF), dtype=jnp.float32) * s
        shared_b2 = jnp.zeros((D_MODEL,), dtype=jnp.float32)
        router_w = jax.random.normal(ks[3], (N_EXPERTS, D_MODEL), dtype=jnp.float32) * s
        router_b = jnp.zeros((N_EXPERTS,), dtype=jnp.float32)
        spec_w1 = jax.random.normal(ks[4], (N_EXPERTS, D_FF, D_MODEL), dtype=jnp.float32) * s
        spec_b1 = jnp.zeros((N_EXPERTS, D_FF), dtype=jnp.float32)
        spec_w2 = jax.random.normal(ks[5], (N_EXPERTS, D_MODEL, D_FF), dtype=jnp.float32) * s
        spec_b2 = jnp.zeros((N_EXPERTS, D_MODEL), dtype=jnp.float32)
        return dict(x=x, shared_w1=shared_w1, shared_b1=shared_b1, shared_w2=shared_w2, shared_b2=shared_b2, router_w=router_w, router_b=router_b, spec_w1=spec_w1, spec_b1=spec_b1, spec_w2=spec_w2, spec_b2=spec_b2)
    _L0_ffn_all = _L0_ffn_setup()
    _L0_ffn_in = {k: v for k, v in _L0_ffn_all.items() if k in ('shared_w1', 'shared_b1', 'shared_w2', 'shared_b2', 'router_w', 'router_b', 'spec_w1', 'spec_b1', 'spec_w2', 'spec_b2')}
    del _L0_ffn_all
    return {'x': x, 'ctx_1024': ctx_1024, 'mask_BxS2_ik0': mask_BxS2_ik0, 'L0_xattn_Wq': _L0_xattn_in['Wq'], 'L0_xattn_bq': _L0_xattn_in['bq'], 'L0_xattn_Wk': _L0_xattn_in['Wk'], 'L0_xattn_bk': _L0_xattn_in['bk'], 'L0_xattn_Wv': _L0_xattn_in['Wv'], 'L0_xattn_bv': _L0_xattn_in['bv'], 'L0_xattn_Wo': _L0_xattn_in['Wo'], 'L0_xattn_bo': _L0_xattn_in['bo'], 'L0_ffn_shared_w1': _L0_ffn_in['shared_w1'], 'L0_ffn_shared_b1': _L0_ffn_in['shared_b1'], 'L0_ffn_shared_w2': _L0_ffn_in['shared_w2'], 'L0_ffn_shared_b2': _L0_ffn_in['shared_b2'], 'L0_ffn_router_w': _L0_ffn_in['router_w'], 'L0_ffn_router_b': _L0_ffn_in['router_b'], 'L0_ffn_spec_w1': _L0_ffn_in['spec_w1'], 'L0_ffn_spec_b1': _L0_ffn_in['spec_b1'], 'L0_ffn_spec_w2': _L0_ffn_in['spec_w2'], 'L0_ffn_spec_b2': _L0_ffn_in['spec_b2']}

def reference(x, ctx_1024, mask_BxS2_ik0, L0_xattn_Wq, L0_xattn_bq, L0_xattn_Wk, L0_xattn_bk, L0_xattn_Wv, L0_xattn_bv, L0_xattn_Wo, L0_xattn_bo, L0_ffn_shared_w1, L0_ffn_shared_b1, L0_ffn_shared_w2, L0_ffn_shared_b2, L0_ffn_router_w, L0_ffn_router_b, L0_ffn_spec_w1, L0_ffn_spec_b1, L0_ffn_spec_w2, L0_ffn_spec_b2):
    import jax
    import jax.numpy as jnp

    def _L0_xattn_ref(q, k, v, mask, Wq, bq, Wk, bk, Wv, bv, Wo, bo):
        import jax, jax.numpy as jnp
        import numpy as np
        EMB_DIM = 128
        NUM_HEADS = 16
        HEAD_DIM = EMB_DIM // NUM_HEADS
        B, S_Q, S_KV = (4, 256, 256)
        Bsz, Sq, E = q.shape
        Skv = k.shape[1]
        H, D = (NUM_HEADS, HEAD_DIM)
        scale = D ** (-0.5)
        qh = (q @ Wq.T + bq).reshape(Bsz, Sq, H, D).transpose(0, 2, 1, 3)
        kh = (k @ Wk.T + bk).reshape(Bsz, Skv, H, D).transpose(0, 2, 1, 3)
        vh = (v @ Wv.T + bv).reshape(Bsz, Skv, H, D).transpose(0, 2, 1, 3)
        attn = jnp.einsum('bhqd,bhkd->bhqk', qh, kh) * scale
        valid = mask != 0
        all_invalid = ~jnp.any(valid, axis=-1, keepdims=True)
        safe = valid | all_invalid
        attn = jnp.where(safe[:, None, None, :], attn, -jnp.inf)
        attn = jax.nn.softmax(attn, axis=-1)
        attn = jnp.where(all_invalid.reshape(Bsz, 1, 1, 1), 0.0, attn)
        out = jnp.einsum('bhqk,bhkd->bhqd', attn, vh)
        out = out.transpose(0, 2, 1, 3).reshape(Bsz, Sq, E)
        return out @ Wo.T + bo

    def _L0_ffn_ref(x, shared_w1, shared_b1, shared_w2, shared_b2, router_w, router_b, spec_w1, spec_b1, spec_w2, spec_b2):
        import jax, jax.numpy as jnp
        import numpy as np
        D_MODEL = 128
        D_FF = 512
        N_EXPERTS = 8
        TOP_K = 2

        def _ffn(x, w1, b1, w2, b2):
            h = jax.nn.gelu(x @ w1.T + b1)
            return h @ w2.T + b2
        B, T, D = x.shape
        xf = x.reshape(-1, D)
        U = xf.shape[0]
        logits = xf @ router_w.T + router_b
        routing = jax.nn.softmax(logits, axis=-1)
        sel_w, sel_idx = jax.lax.top_k(routing, TOP_K)
        sel_w = sel_w / sel_w.sum(axis=-1, keepdims=True)
        comb = jnp.zeros_like(routing).at[jnp.arange(U)[:, None], sel_idx].set(sel_w)
        shared_out = _ffn(xf, shared_w1, shared_b1, shared_w2, shared_b2)

        def body(acc, params):
            w1, b1, w2, b2, we = params
            return (acc + we[:, None] * _ffn(xf, w1, b1, w2, b2), None)
        acc0 = jnp.zeros_like(shared_out)
        acc, _ = jax.lax.scan(body, acc0, (spec_w1, spec_b1, spec_w2, spec_b2, comb.T))
        return (shared_out + acc).reshape(B, T, D)
    x = x + _L0_xattn_ref(_layernorm(x, axis=-1), ctx_1024, ctx_1024, mask_BxS2_ik0, L0_xattn_Wq, L0_xattn_bq, L0_xattn_Wk, L0_xattn_bk, L0_xattn_Wv, L0_xattn_bv, L0_xattn_Wo, L0_xattn_bo)
    x = x + _L0_ffn_ref(_layernorm(x, axis=-1), L0_ffn_shared_w1, L0_ffn_shared_b1, L0_ffn_shared_w2, L0_ffn_shared_b2, L0_ffn_router_w, L0_ffn_router_b, L0_ffn_spec_w1, L0_ffn_spec_b1, L0_ffn_spec_w2, L0_ffn_spec_b2)
    return x

_drawn_inputs = setup_inputs


def setup_inputs(seed=0):
    import zlib

    import numpy as np

    out = dict(_drawn_inputs(seed))
    spreads = {'L0_xattn_bq': (0.0, 0.358),
     'L0_xattn_bk': (0.0, 0.8),
     'L0_xattn_bv': (0.0, 0.1),
     'L0_xattn_bo': (0.0, 0.1),
     'L0_ffn_shared_b1': (0.0, 0.416),
     'L0_ffn_shared_b2': (0.0, 0.1),
     'L0_ffn_router_b': (0.0, 0.1),
     'L0_ffn_spec_b1': (0.0, 0.541),
     'L0_ffn_spec_b2': (0.0, 0.1)}
    factors = {}
    for name, (base, spread) in spreads.items():
        noise = np.random.default_rng([zlib.crc32(name.encode()), seed]).standard_normal(out[name].shape)
        drawn = base * np.exp(spread * noise) if base else spread * noise
        out[name] = jnp.asarray(drawn.astype(out[name].dtype))
    for name, factor in factors.items():
        out[name] = (out[name] * factor).astype(out[name].dtype)
    return out
```

```python
from contextlib import ExitStack

import concourse.bass as bass
from concourse import mybir

ALU = mybir.AluOpType
ACT = mybir.ActivationFunctionType
F32 = mybir.dt.float32
F32R = mybir.dt.float32r
I32 = mybir.dt.int32
U32 = mybir.dt.uint32
AX_X = mybir.AxisListType.X

P = 128
HEADS, HD = 16, 8
NEG = -1e30
EPS = 1e-5

C_WK, C_WV, C_WQ, C_WO = 0, P, 2 * P, 3 * P
C_CTX = 4 * P


def xattn_moe_kernel(nc, x, params, rows, mask, experts, out):
    B, S, D = x.shape
    KEYS = mask.shape[1] // B
    HK = HEADS * KEYS
    T = S // P
    NT = B * T
    NE = experts.shape[0]
    R = NE - 1
    F = experts.shape[2] // 2
    FC = F // P
    HC = HK // P
    SCALE = float(HD) ** -0.5
    C_BQ = C_CTX + B * KEYS
    C_BK, C_BV = C_BQ + 1, C_BQ + 2
    C_WR = C_BQ + 3
    C_B1 = C_WR + R
    C_B2 = C_B1 + NE * FC
    assert params.shape[1] == C_B2 + NE and S == 512 and D == P and HK == 512 and R % 2 == 0

    combt_dram = nc.dram_tensor("combt_scratch", [R, B, S], F32, kind="Internal").ap()

    with ExitStack() as ctx:
        def sb(name, shape, dt=F32):
            return ctx.enter_context(nc.sbuf_tensor(name, shape, dt))

        def sem(name):
            return ctx.enter_context(nc.semaphore(name))

        par = sb("par", [P, C_B2 + NE])
        rowb = sb("rowb", [P, P + R])
        maskb = sb("maskb", [P, B * KEYS], I32)
        ident = sb("ident", [P, P])
        headmask = sb("headmask", [P, HEADS, KEYS])
        iota8 = sb("iota8", [P, R])
        neghalf = sb("neghalf", [P, T])
        xin = sb("xin", [P, B, T, P])
        xb = sb("xb", [P, B, T, P])
        x2 = sb("x2", [P, B, T, P])
        xn = sb("xn", [P, B, T, P])
        stats = sb("stats", [P, T, 6])
        mv = sb("mv", [P, 2, B, T, 2])
        vareps = sb("vareps", [P, 2, B, T])
        rstd = sb("rstd", [P, 2, B, T])
        xt_hi = [sb(f"xt{k}_hi", [P, B, T * P], F32R) for k in range(2)]
        xt_lo = [sb(f"xt{k}_lo", [P, B, T * P], F32R) for k in range(2)]
        kv = sb("kv", [P, 2, B * KEYS])
        kbd = sb("kbd", [P, B, HEADS, KEYS])
        vbd = sb("vbd", [P, B, HEADS, KEYS])
        m_hi = sb("m_hi", [P, B, HK], F32R)
        m_lo = sb("m_lo", [P, B, HK], F32R)
        vw = sb("vw", [P, B, HC, P])
        isvalid = sb("isvalid", [P, B * KEYS])
        anyvalid = sb("anyvalid", [P, B])
        brow = sb("brow", [65, B, HK], F32R)
        ones_r = sb("ones_r", [65, P], F32R)
        wr_hi = sb("wr_hi", [P, R], F32R)
        wr_lo = sb("wr_lo", [P, R], F32R)
        rowmax = sb("rowmax", [P, 2, HEADS])
        shifted = sb("shifted", [P, 2, HK])
        probs = sb("probs", [P, 2, HK])
        rowsum = sb("rowsum", [P, 2, HEADS])
        rrow = sb("rrow", [P, 2, HEADS])
        probn = sb("probn", [P, 2, HK])
        probt = sb("probt", [P, 2, HK])
        logits = sb("logits", [P, B, T, R])
        top8 = sb("top8", [P, B, T, 8])
        idx8 = sb("idx8", [P, B, T, 8], U32)
        idxf = sb("idxf", [P, B, T, 2])
        gap = sb("gap", [P, B, T])
        w12 = sb("w12", [P, B, T, 2])
        den = sb("den", [P, B, T])
        e21 = sb("e21", [P, B, T])
        hot = sb("hot", [P, B, T, 2, R])
        hotw = sb("hotw", [P, B, T, 2, R])
        comb = sb("comb", [P, B, T, R])
        combt = sb("combt", [R, B, T * P])
        combb = sb("combb", [P, 2, B, S])
        wst = sb("wst", [P, 2, 2 * F])
        w_hi = [sb(f"w_hi{s}", [P, 2 * F], F32R) for s in range(2)]
        w_lo = [sb(f"w_lo{s}", [P, 2 * F], F32R) for s in range(2)]
        b1cur = sb("b1cur", [P, 2, FC])
        h_full = sb("h_full", [P, FC, B * S])
        h_hi = sb("h_hi", [P, FC, B * S], F32R)
        h_lo = sb("h_lo", [P, FC, B * S], F32R)
        scaled = sb("scaled", [P, B, S])
        acc = sb("acc", [P, B, S])
        fin = sb("fin", [P, B, T, P])

        ps = [ctx.enter_context(nc.psum_tensor(f"bank{i}", [P, 1024], F32)) for i in range(4)]

        def bank(i):
            return ps[i // 2][:, 512 * (i % 2):512 * (i % 2) + 512]

        SCO = (1, 2)
        PTR = (3, 4)
        YBK = (5, 6)

        params_in, biases_in, rows_in, mask_in = sem("params_in"), sem("biases_in"), sem("rows_in"), sem("mask_in")
        x_in = [sem(f"x_in{b}") for b in range(B)]
        ident_ready, headmask_ready, consts_ready = sem("ident_ready"), sem("headmask_ready"), sem("consts_ready")
        iota_ready = sem("iota_ready")
        xb_ready = sem("xb_ready")
        kv_psum, kv_ready, bd_ready = sem("kv_psum"), sem("kv_ready"), sem("bd_ready")
        m_psum, m_hi_ready, m_ready = sem("m_psum"), sem("m_hi_ready"), sem("m_ready")
        cb_psum, cb_hi_ready, cb_ready = sem("cb_psum"), sem("cb_hi_ready"), sem("cb_ready")
        wr_ready = sem("wr_ready")
        brow_zero, valid_ready, any_ready, maskrow_ready = (
            sem("brow_zero"), sem("valid_ready"), sem("any_ready"), sem("maskrow_ready"))
        vw_psum, vw_ready = sem("vw_psum"), sem("vw_ready")
        st_done = [sem(f"ln{k}_stats") for k in range(2)]
        mv_done = [sem(f"ln{k}_meanvar") for k in range(2)]
        ve_done = [sem(f"ln{k}_vareps") for k in range(2)]
        rs_done = [sem(f"ln{k}_rstd") for k in range(2)]
        xn_done = [sem(f"ln{k}_normed") for k in range(2)]
        tr_done = [sem(f"ln{k}_transposed") for k in range(2)]
        xhi_done = [sem(f"ln{k}_hi") for k in range(2)]
        xlo_done = [sem(f"ln{k}_lo") for k in range(2)]
        scores_done, max_done, shift_done, exp_done = (
            sem("scores_done"), sem("max_done"), sem("shift_done"), sem("exp_done"))
        sum_done, recip_done, probn_done, ptr_done, probt_done, y_done, x2_done = (
            sem("sum_done"), sem("recip_done"), sem("probn_done"), sem("ptr_done"),
            sem("probt_done"), sem("y_done"), sem("x2_done"))
        logit_psum, logit_ready, top_ready, idx_ready, idxf_ready = (
            sem("logit_psum"), sem("logit_ready"), sem("top_ready"), sem("idx_ready"), sem("idxf_ready"))
        gap_ready, e21_ready, den_ready, w1_ready, w2_ready = (
            sem("gap_ready"), sem("e21_ready"), sem("den_ready"), sem("w1_ready"), sem("w2_ready"))
        hot_ready, hotw_ready, comb_ready = sem("hot_ready"), sem("hotw_ready"), sem("comb_ready")
        combt_psum, combt_ready, combt_stored = sem("combt_psum"), sem("combt_ready"), sem("combt_stored")
        comb_in = [sem(f"comb_in{s}") for s in range(2)]
        w_in = [sem(f"w_in{s}") for s in range(2)]
        whi_done, wlo_done = sem("whi_done"), sem("wlo_done")
        b1_ready = sem("b1_ready")
        up_done, gelu_done, hhi_done, hlo_done, down_done = (
            sem("up_done"), sem("gelu_done"), sem("hhi_done"), sem("hlo_done"), sem("down_done"))
        scaled_done, acc_done = sem("scaled_done"), sem("acc_done")
        back_done, fin_done, out_stored = sem("back_done"), sem("fin_done"), sem("out_stored")

        block = ctx.enter_context(nc.Block())

        @block.sync
        def _(sp):
            sp.dma_start(par[:, 0:C_B1], params[:, 0:C_B1]).then_inc(params_in, 16)
            sp.dma_start(xin[:, 1], x[1].rearrange("(p t) d -> p t d", t=T)).then_inc(x_in[1], 16)

            def load_weights(e, s):
                sp.dma_start(wst[:, s], experts[e]).then_inc(w_in[s], 16)

            def load_comb(e, s):
                sp.dma_start(combb[:, s], combt_dram[e - 1].partition_broadcast(P)).then_inc(comb_in[s], 16)

            load_weights(0, 0)
            load_weights(1, 1)
            sp.dma_start(par[:, C_B1:C_B2 + NE], params[:, C_B1:C_B2 + NE]).then_inc(biases_in, 16)
            sp.wait_ge(wlo_done, 1)
            sp.wait_ge(whi_done, 1)
            load_weights(2, 0)
            for b in range(B):
                sp.wait_ge(combt_ready, b + 1)
                sp.dma_start(combt_dram[:, b], combt[:, b]).then_inc(combt_stored, 16)
            sp.wait_ge(combt_stored, 16 * B)
            load_comb(1, 1)
            load_comb(2, 0)
            with sp.Fori(0, R // 2 - 1) as i:
                e = i * 2 + 1
                sp.wait_ge(wlo_done, e + 1)
                sp.wait_ge(whi_done, e + 1)
                load_weights(e + 2, 1)
                sp.wait_ge(scaled_done, B * e)
                load_comb(e + 2, 1)
                sp.wait_ge(wlo_done, e + 2)
                sp.wait_ge(whi_done, e + 2)
                load_weights(e + 3, 0)
                sp.wait_ge(scaled_done, B * (e + 1))
                load_comb(e + 3, 0)
            for b in range(B):
                sp.wait_ge(fin_done, b + 1)
                sp.dma_start(out[b].rearrange("(p t) d -> p t d", t=T), fin[:, b]).then_inc(out_stored, 16)
            sp.wait_ge(out_stored, 16 * B)

        @block.gpsimd
        def _(pool):
            pool.memset(ident[:], 0.0).then_inc(ident_ready, 1)
            pool.memset(headmask[:], 1.0).then_inc(headmask_ready, 1)
            pool.memset(neghalf[:], -0.5).then_inc(consts_ready, 1)
            pool.wait_ge(ident_ready, 1)
            pool.affine_select(out=ident[:], in_=ident[:], compare_op=ALU.not_equal, fill=1.0, base=0,
                               pattern=[[-1, P]], channel_multiplier=1).then_inc(ident_ready, 1)
            pool.wait_ge(headmask_ready, 1)
            pool.affine_select(out=headmask[:], in_=headmask[:], compare_op=ALU.is_ge, fill=0.0, base=0,
                               pattern=[[-HD, HEADS], [0, KEYS]], channel_multiplier=1).then_inc(headmask_ready, 1)
            pool.wait_ge(headmask_ready, 2)
            pool.affine_select(out=headmask[:], in_=headmask[:], compare_op=ALU.is_ge, fill=0.0, base=HD - 1,
                               pattern=[[HD, HEADS], [0, KEYS]], channel_multiplier=-1).then_inc(headmask_ready, 1)
            pool.iota(iota8[:], pattern=[[1, R]], base=0, channel_multiplier=0,
                      allow_small_or_imprecise_dtypes=True).then_inc(iota_ready, 1)

            def rstd_of(k, b):
                pool.wait_ge(ve_done[k], b + 1)
                pool.tensor_tensor(rstd[:, k, b], vareps[:, k, b], neghalf[:], ALU.pow).then_inc(rs_done[k], 1)

            pool.wait_ge(consts_ready, 1)
            for b in range(B):
                rstd_of(0, b)
            pool.wait_ge(rows_in, 16)
            for b in range(B):
                pool.wait_ge(x_in[b], 16)
                pool.tensor_tensor(xb[:, b], xin[:, b],
                                   rowb[:, 0:P].unsqueeze(1).broadcast_to([P, T, P]),
                                   ALU.add).then_inc(xb_ready, 1)

            def normalise(i):
                s = i % 2
                pool.wait_ge(recip_done, i + 1)
                if i >= 2:
                    pool.wait_ge(ptr_done, i - 1)
                pool.tensor_tensor(probn[:, s].rearrange("p (h k) -> p h k", h=HEADS),
                                   probs[:, s].rearrange("p (h k) -> p h k", h=HEADS),
                                   rrow[:, s].unsqueeze(2).broadcast_to([P, HEADS, KEYS]),
                                   ALU.mult).then_inc(probn_done, 1)

            def split_w_lo(e, s):
                pool.wait_ge(whi_done, e + 1)
                pool.tensor_tensor(w_lo[s][:], wst[:, s], w_hi[s][:].bitcast(F32), ALU.subtract).then_inc(wlo_done, 1)

            for i in range(NT):
                normalise(i)
                if i in (3, 4):
                    split_w_lo(i - 3, i - 3)
                if i == T + 1:
                    rstd_of(1, 0)
            rstd_of(1, 1)

            def accumulate(e):
                for b in range(B):
                    pool.wait_ge(scaled_done, B * (e - 1) + b + 1)
                    pool.wait_ge(acc_done, B * (e - 1) + b + 1)
                    pool.tensor_tensor(acc[:, b], acc[:, b], scaled[:, b], ALU.add).then_inc(acc_done, 1)

            split_w_lo(2, 0)
            with pool.Fori(0, R // 2 - 1) as i:
                e = i * 2 + 1
                accumulate(e)
                split_w_lo(e + 2, 1)
                accumulate(e + 1)
                split_w_lo(e + 3, 0)
            accumulate(NE - 2)
            accumulate(NE - 1)

        @block.scalar
        def _(act):
            act.dma_start(xin[:, 0], x[0].rearrange("(p t) d -> p t d", t=T)).then_inc(x_in[0], 16)
            act.dma_start(maskb[:], mask.partition_broadcast(P)).then_inc(mask_in, 16)
            act.dma_start(rowb[:], rows.partition_broadcast(P)).then_inc(rows_in, 16)

            def xt_high(k, b):
                act.wait_ge(tr_done[k], b + 1)
                act.activation(xt_hi[k][:, b], bank(0), ACT.Copy).then_inc(xhi_done[k], 1)

            for b in range(B):
                act.wait_ge(m_psum, b + 1)
                act.activation(m_hi[:, b], bank(1 + b), ACT.Copy, scale=SCALE).then_inc(m_hi_ready, 1)
            xt_high(0, 0)
            for b in range(B):
                act.wait_ge(cb_psum, b + 1)
                act.wait_ge(brow_zero, 1)
                act.activation(brow[0:1, b], bank(3 + b)[0:1], ACT.Copy, scale=SCALE).then_inc(cb_hi_ready, 1)
            xt_high(0, 1)

            def exp(i):
                act.wait_ge(shift_done, i + 1)
                if i >= 2:
                    act.wait_ge(probn_done, i - 1)
                    act.wait_ge(sum_done, i - 1)
                act.activation(probs[:, i % 2], shifted[:, i % 2], ACT.Exp).then_inc(exp_done, 1)

            def copy_probt(i):
                act.wait_ge(ptr_done, i + 1)
                if i >= 2:
                    act.wait_ge(y_done, i - 1)
                act.activation(probt[:, i % 2], bank(PTR[i % 2]), ACT.Copy).then_inc(probt_done, 1)

            def router_exp(b):
                act.wait_ge(gap_ready, b + 1)
                act.activation(e21[:, b], gap[:, b], ACT.Exp).then_inc(e21_ready, 1)

            def copy_combt(b):
                act.wait_ge(combt_psum, b + 1)
                act.activation(combt[:, b], bank(7)[0:R], ACT.Copy).then_inc(combt_ready, 1)

            for i in range(NT + 1):
                if i < NT:
                    exp(i)
                if i >= 1:
                    copy_probt(i - 1)
                if i == T + 2:
                    xt_high(1, 0)
            router_exp(0)
            copy_combt(0)
            xt_high(1, 1)
            router_exp(1)
            copy_combt(1)

            def take_b1(e, s):
                act.activation(b1cur[:, s], par[:, bass.ds(C_B1 + e * FC, FC)], ACT.Copy).then_inc(b1_ready, 1)

            def gelu(e, s, f, first=False):
                u = ps[f % 2][:]
                b1 = b1cur[:, s, f:f + 1]
                act.wait_ge(b1_ready, e + 1)
                act.wait_ge(up_done, e * FC + (f + 1))
                if not first:
                    act.wait_ge(hlo_done, (e - 1) * FC + (f + 1))
                act.activation(h_full[:, f], u, ACT.Gelu_apprx_tanh, bias=b1).then_inc(gelu_done, 1)
                if not first:
                    act.wait_ge(down_done, (e - 1) * FC + (f + 1))
                act.activation(h_hi[:, f], u, ACT.Gelu_apprx_tanh, bias=b1).then_inc(hhi_done, 1)

            act.wait_ge(biases_in, 16)
            take_b1(0, 0)
            for f in range(FC):
                gelu(0, 0, f, True)
            take_b1(1, 1)
            with act.Fori(0, R // 2 - 1) as i:
                e = i * 2 + 1
                for f in range(FC):
                    gelu(e, 1, f)
                take_b1(e + 1, 0)
                for f in range(FC):
                    gelu(e + 1, 0, f)
                take_b1(e + 2, 1)
            for f in range(FC):
                gelu(R - 1, 1, f)
            take_b1(R, 0)
            for f in range(FC):
                gelu(R, 0, f)

        @block.vector
        def _(dve):
            dve.memset(brow[:].bitcast(F32), 0.0).then_inc(brow_zero, 1)
            dve.memset(ones_r[:].bitcast(F32), 1.0).then_inc(brow_zero, 1)

            def meanvar(k, b, src):
                for t in range(T):
                    dve.bn_stats(stats[:, t], src[:, b, t]).then_inc(st_done[k], 1)
                for t in range(T):
                    dve.wait_ge(st_done[k], T * b + t + 1)
                    dve.bn_aggr(mv[:, k, b, t], stats[:, t]).then_inc(mv_done[k], 1)
                dve.wait_ge(mv_done[k], T * (b + 1))
                dve.tensor_scalar(vareps[:, k, b], mv[:, k, b, :, 1], EPS, None, ALU.add).then_inc(ve_done[k], 1)

            def norm(k, b, src):
                dve.wait_ge(rs_done[k], b + 1)
                if k == 1 and b == 0:
                    pass
                for t in range(T):
                    dve.tensor_scalar(xn[:, b, t], src[:, b, t], mv[:, k, b, t, 0:1], rstd[:, k, b, t:t + 1],
                                      ALU.subtract, ALU.mult).then_inc(xn_done[k], 1)

            def xt_low(k, b):
                dve.wait_ge(xhi_done[k], b + 1)
                dve.tensor_tensor(xt_lo[k][:, b], bank(0), xt_hi[k][:, b].bitcast(F32),
                                  ALU.subtract).then_inc(xlo_done[k], 1)

            dve.wait_ge(x_in[0], 16)
            meanvar(0, 0, xin)
            for n, c in enumerate((C_BK, C_BV)):
                dve.wait_ge(kv_psum, 1)
                dve.tensor_scalar(kv[:, n], bank(7)[:, n * B * KEYS:(n + 1) * B * KEYS], par[:, c:c + 1], None,
                                  ALU.add).then_inc(kv_ready, 1)
            norm(0, 0, xin)
            dve.tensor_copy(wr_hi[:], par[:, C_WR:C_WR + R]).then_inc(wr_ready, 1)
            dve.wait_ge(headmask_ready, 3)
            dve.wait_ge(kv_ready, 2)
            for n, bd in enumerate((kbd, vbd)):
                for b in range(B):
                    dve.tensor_tensor(bd[:, b], headmask[:],
                                      kv[:, n, b * KEYS:(b + 1) * KEYS].unsqueeze(1).broadcast_to([P, HEADS, KEYS]),
                                      ALU.mult).then_inc(bd_ready, 1)
            dve.wait_ge(wr_ready, 1)
            dve.tensor_tensor(wr_lo[:], par[:, C_WR:C_WR + R], wr_hi[:].bitcast(F32),
                              ALU.subtract).then_inc(wr_ready, 1)
            dve.wait_ge(x_in[1], 16)
            meanvar(0, 1, xin)
            dve.wait_ge(mask_in, 16)
            dve.tensor_scalar(isvalid[:], maskb[:], 0.0, None, ALU.not_equal).then_inc(valid_ready, 1)
            dve.wait_ge(valid_ready, 1)
            dve.tensor_reduce(anyvalid[:], isvalid[:].rearrange("p (b k) -> p b k", b=B), AX_X,
                              ALU.max).then_inc(any_ready, 1)
            dve.wait_ge(brow_zero, 2)
            for b in range(B):
                dve.tensor_scalar(brow[64:65, b].rearrange("p (h k) -> p h k", h=HEADS),
                                  isvalid[64:65, b * KEYS:(b + 1) * KEYS].unsqueeze(1).broadcast_to([1, HEADS, KEYS]),
                                  -NEG, NEG, ALU.mult, ALU.add).then_inc(maskrow_ready, 1)
            for b in range(B):
                dve.wait_ge(m_hi_ready, b + 1)
                dve.scalar_tensor_tensor(out=m_lo[:, b], in0=bank(1 + b), scalar=SCALE, in1=m_hi[:, b].bitcast(F32),
                                         op0=ALU.mult, op1=ALU.subtract).then_inc(m_ready, 1)
            xt_low(0, 0)
            norm(0, 1, xin)
            for b in range(B):
                dve.wait_ge(cb_hi_ready, b + 1)
                dve.scalar_tensor_tensor(out=brow[32:33, b], in0=bank(3 + b)[0:1], scalar=SCALE,
                                         in1=brow[0:1, b].bitcast(F32),
                                         op0=ALU.mult, op1=ALU.subtract).then_inc(cb_ready, 1)
            dve.wait_ge(any_ready, 1)
            for b in range(B):
                dve.wait_ge(vw_psum, b + 1)
                dve.tensor_scalar(vw[:, b].rearrange("p c d -> p (c d)"), bank(5 + b), anyvalid[:, b:b + 1], None,
                                  ALU.mult).then_inc(vw_ready, 1)
            xt_low(0, 1)

            def heads(ap):
                return ap.rearrange("p (h k) -> p h k", h=HEADS)

            def shift(i):
                s = i % 2
                sc = heads(bank(SCO[s]))
                dve.wait_ge(scores_done, i + 1)
                dve.tensor_reduce(rowmax[:, s], sc, AX_X, ALU.max).then_inc(max_done, 1)
                dve.wait_ge(max_done, i + 1)
                if i >= 2:
                    dve.wait_ge(exp_done, i - 1)
                dve.tensor_tensor(heads(shifted[:, s]), sc,
                                  rowmax[:, s].unsqueeze(2).broadcast_to([P, HEADS, KEYS]),
                                  ALU.subtract).then_inc(shift_done, 1)

            def row_sums(i):
                s = i % 2
                dve.wait_ge(exp_done, i + 1)
                dve.tensor_reduce(rowsum[:, s], heads(probs[:, s]), AX_X, ALU.add).then_inc(sum_done, 1)
                dve.wait_ge(sum_done, i + 1)
                if i >= 2:
                    dve.wait_ge(probn_done, i - 1)
                dve.reciprocal(rrow[:, s], rowsum[:, s]).then_inc(recip_done, 1)

            def residual(i):
                dve.wait_ge(y_done, i + 1)
                dve.wait_ge(xb_ready, i // T + 1)
                dve.tensor_tensor(x2[:, i // T, i % T], bank(YBK[i % 2])[:, 0:P], xb[:, i // T, i % T],
                                  ALU.add).then_inc(x2_done, 1)

            def route(b):
                dve.wait_ge(logit_psum, b + 1)
                dve.tensor_tensor(logits[:, b], bank(7)[:, 0:T * R].rearrange("p (t e) -> p t e", t=T),
                                  rowb[:, P:P + R].unsqueeze(1).broadcast_to([P, T, R]),
                                  ALU.add).then_inc(logit_ready, 1)
                dve.wait_ge(logit_ready, b + 1)
                for t in range(T):
                    dve.max(top8[:, b, t], logits[:, b, t]).then_inc(top_ready, 1)
                dve.wait_ge(top_ready, T * (b + 1))
                for t in range(T):
                    dve.max_index(idx8[:, b, t], top8[:, b, t], logits[:, b, t]).then_inc(idx_ready, 1)
                dve.tensor_tensor(gap[:, b], top8[:, b, :, 1], top8[:, b, :, 0], ALU.subtract).then_inc(gap_ready, 1)
                dve.wait_ge(idx_ready, T * (b + 1))
                dve.tensor_copy(idxf[:, b], idx8[:, b, :, 0:2]).then_inc(idxf_ready, 1)
                dve.wait_ge(idxf_ready, b + 1)
                dve.wait_ge(iota_ready, 1)
                dve.tensor_tensor(hot[:, b],
                                  iota8[:].unsqueeze(1).unsqueeze(1).broadcast_to([P, T, 2, R]),
                                  idxf[:, b].unsqueeze(3).broadcast_to([P, T, 2, R]),
                                  ALU.is_equal).then_inc(hot_ready, 1)
                dve.wait_ge(e21_ready, b + 1)
                dve.tensor_scalar(den[:, b], e21[:, b], 1.0, None, ALU.add).then_inc(den_ready, 1)
                dve.wait_ge(den_ready, b + 1)
                dve.reciprocal(w12[:, b, :, 0], den[:, b]).then_inc(w1_ready, 1)
                dve.wait_ge(w1_ready, b + 1)
                dve.tensor_tensor(w12[:, b, :, 1], w12[:, b, :, 0], e21[:, b], ALU.mult).then_inc(w2_ready, 1)
                dve.wait_ge(w2_ready, b + 1)
                dve.wait_ge(hot_ready, b + 1)
                dve.tensor_tensor(hotw[:, b], hot[:, b], w12[:, b].unsqueeze(3).broadcast_to([P, T, 2, R]),
                                  ALU.mult).then_inc(hotw_ready, 1)
                dve.wait_ge(hotw_ready, b + 1)
                dve.tensor_tensor(comb[:, b], hotw[:, b, :, 0], hotw[:, b, :, 1], ALU.add).then_inc(comb_ready, 1)

            def split_w_hi(e, s, first=False):
                dve.wait_ge(w_in[s], 16 * (e // 2 + 1) if isinstance(e, int) else e * 8 + (16 if s == 0 else 8))
                if not first:
                    dve.wait_ge(down_done, FC * (e - 1))
                dve.tensor_copy(w_hi[s][:], wst[:, s]).then_inc(whi_done, 1)

            for i in range(NT + 2):
                if i < NT:
                    shift(i)
                if i in (1, 2):
                    split_w_hi(i - 1, i - 1, True)
                if 1 <= i <= NT:
                    row_sums(i - 1)
                if i >= 2:
                    residual(i - 2)
                    if i - 2 == T - 1:
                        dve.wait_ge(x2_done, T)
                        meanvar(1, 0, x2)
                    if i - 2 == T:
                        norm(1, 0, x2)
                    if i - 2 == T + 1:
                        xt_low(1, 0)
            dve.wait_ge(x2_done, 2 * T)
            meanvar(1, 1, x2)
            route(0)
            norm(1, 1, x2)
            xt_low(1, 1)
            route(1)

            def h_low(e, f, first=False):
                dve.wait_ge(gelu_done, e * FC + (f + 1))
                dve.wait_ge(hhi_done, e * FC + (f + 1))
                dve.tensor_tensor(h_lo[:, f], h_full[:, f], h_hi[:, f].bitcast(F32),
                                  ALU.subtract).then_inc(hlo_done, 1)

            def weigh(e, s, comb_value):
                b2 = par[:, bass.ds(C_B2 + e, 1)]
                dve.wait_ge(down_done, e * FC + FC)
                dve.wait_ge(comb_in[s], comb_value)
                for b in range(B):
                    dve.wait_ge(acc_done, B * (e - 1) + b + 1)
                    dve.scalar_tensor_tensor(out=scaled[:, b], in0=ps[2 + s][:, b * S:(b + 1) * S], scalar=b2,
                                             in1=combb[:, s, b], op0=ALU.add, op1=ALU.mult).then_inc(scaled_done, 1)

            for f in range(FC):
                h_low(0, f, True)
            dve.wait_ge(down_done, FC)
            dve.wait_ge(biases_in, 16)
            for b in range(B):
                dve.tensor_scalar(acc[:, b], ps[2][:, b * S:(b + 1) * S], par[:, C_B2:C_B2 + 1], None,
                                  ALU.add).then_inc(acc_done, 1)
            split_w_hi(2, 0)
            with dve.Fori(0, R // 2 - 1) as i:
                e = i * 2 + 1
                for f in range(FC):
                    h_low(e, f)
                weigh(e, 1, e * 8 + 8)
                split_w_hi(e + 2, 1)
                for f in range(FC):
                    h_low(e + 1, f)
                weigh(e + 1, 0, e * 8 + 8)
                split_w_hi(e + 3, 0)
            for e in (NE - 2, NE - 1):
                for f in range(FC):
                    h_low(e, f)
                weigh(e, e % 2, 16 * ((e - 1) // 2 + 1))
            for b in range(B):
                dve.wait_ge(back_done, b + 1)
                dve.tensor_tensor(fin[:, b].rearrange("p t d -> p (t d)"), bank(b),
                                  x2[:, b].rearrange("p t d -> p (t d)"), ALU.add).then_inc(fin_done, 1)

        @block.tensor
        def _(pe):
            def transpose_norm(k, b):
                for t in range(T):
                    pe.wait_ge(xn_done[k], T * b + t + 1)
                    mm = pe.transpose(bank(0)[:, t * P:(t + 1) * P], xn[:, b, t], ident[:])
                mm.then_inc(tr_done[k], 1)

            pe.wait_ge(params_in, 16)
            for n, c in enumerate((C_WK, C_WV)):
                mm = pe.matmul(bank(7)[:, n * B * KEYS:(n + 1) * B * KEYS], par[:, c:c + P],
                               par[:, C_CTX:C_CTX + B * KEYS], start=True, stop=True)
            mm.then_inc(kv_psum, 1)
            pe.wait_ge(ident_ready, 2)
            transpose_norm(0, 0)
            for b in range(B):
                pe.wait_ge(bd_ready, b + 1)
                pe.matmul(bank(1 + b), par[:, C_WQ:C_WQ + P], kbd[:, b].rearrange("p h k -> p (h k)"),
                          start=True, stop=True).then_inc(m_psum, 1)
            for b in range(B):
                pe.matmul(bank(3 + b)[0:1], par[:, C_BQ:C_BQ + 1], kbd[:, b].rearrange("p h k -> p (h k)"),
                          start=True, stop=True).then_inc(cb_psum, 1)
            pe.wait_ge(bd_ready, 2 * B)
            for b in range(B):
                v = vbd[:, b].rearrange("p h k -> p (h k)")
                for c in range(HC):
                    mm = pe.matmul(bank(5 + b)[:, c * P:(c + 1) * P], v[:, c * P:(c + 1) * P],
                                   par[:, C_WO:C_WO + P], start=True, stop=True)
                mm.then_inc(vw_psum, 1)
            pe.wait_ge(xlo_done[0], 1)
            transpose_norm(0, 1)

            def scores(i):
                b, t = divmod(i, T)
                if i < 2:
                    pe.wait_ge(m_ready, B)
                    pe.wait_ge(cb_ready, B)
                    pe.wait_ge(maskrow_ready, B)
                else:
                    pe.wait_ge(shift_done, i - 1)
                pe.wait_ge(xlo_done[0], b + 1)
                xh, xl = (a[0][:, b, t * P:(t + 1) * P] for a in (xt_hi, xt_lo))
                o = bank(SCO[i % 2])
                pe.matmul(o, ones_r[:], brow[:, b], start=True, stop=False)
                pe.matmul(o, xh, m_lo[:, b], start=False, stop=False)
                pe.matmul(o, xl, m_hi[:, b], start=False, stop=False)
                pe.matmul(o, xh, m_hi[:, b], start=False, stop=True).then_inc(scores_done, 1)

            def transpose_probs(i):
                pe.wait_ge(probn_done, i + 1)
                if i >= 2:
                    pe.wait_ge(probt_done, i - 1)
                for c in range(HC):
                    mm = pe.transpose(bank(PTR[i % 2])[:, c * P:(c + 1) * P], probn[:, i % 2, c * P:(c + 1) * P],
                                      ident[:])
                mm.then_inc(ptr_done, 1)

            def attend(i):
                pe.wait_ge(probt_done, i + 1)
                if i < 2:
                    pe.wait_ge(vw_ready, B)
                else:
                    pe.wait_ge(x2_done, i - 1)
                for c in range(HC):
                    mm = pe.matmul(bank(YBK[i % 2])[:, 0:P], probt[:, i % 2, c * P:(c + 1) * P],
                                   vw[:, i // T, c], start=(c == 0), stop=(c == HC - 1))
                mm.then_inc(y_done, 1)

            def router(b):
                pe.wait_ge(xlo_done[1], b + 1)
                pe.wait_ge(wr_ready, 2)
                if b:
                    pe.wait_ge(combt_ready, b)
                for t in range(T):
                    parts = [a[1][:, b, t * P:(t + 1) * P] for a in (xt_lo, xt_hi)]
                    for n in range(4):
                        mm = pe.matmul(bank(7)[:, t * R:(t + 1) * R], parts[n // 2], (wr_lo, wr_hi)[n % 2][:],
                                       start=(n == 0), stop=(n == 3))
                mm.then_inc(logit_psum, 1)

            def transpose_comb(b):
                pe.wait_ge(comb_ready, b + 1)
                for t in range(T):
                    mm = pe.transpose(bank(7)[0:R, t * P:(t + 1) * P], comb[:, b, t], ident[:])
                mm.then_inc(combt_psum, 1)

            for i in range(NT + 2):
                if i < NT:
                    scores(i)
                if 1 <= i <= NT:
                    transpose_probs(i - 1)
                if i >= 2:
                    attend(i - 2)
                if i - 2 == T:
                    transpose_norm(1, 0)
            router(0)
            transpose_comb(0)
            pe.wait_ge(xlo_done[1], 1)
            transpose_norm(1, 1)
            router(1)
            transpose_comb(1)

            def up(e, s, f, first=False):
                if not first:
                    pe.wait_ge(hhi_done, e * FC + (f - 1))
                wh, wl = (w[s][:, f * P:(f + 1) * P] for w in (w_hi, w_lo))
                for b in range(B):
                    o = ps[f % 2][:, b * S:(b + 1) * S]
                    xh, xl = xt_hi[1][:, b], xt_lo[1][:, b]
                    pe.matmul(o, wl, xh, start=True, stop=False)
                    pe.matmul(o, wh, xl, start=False, stop=False)
                    mm = pe.matmul(o, wh, xh, start=False, stop=True)
                mm.then_inc(up_done, 1)

            def down(e, s, f):
                pe.wait_ge(hlo_done, e * FC + (f + 1))
                if f == 0 and not isinstance(e, int):
                    pe.wait_ge(acc_done, B * (e - 1) + 1)
                wh, wl = (w[s][:, F + f * P:F + (f + 1) * P] for w in (w_hi, w_lo))
                for b in range(B):
                    o = ps[2 + s][:, b * S:(b + 1) * S]
                    hh, hl = (h[:, f, b * S:(b + 1) * S] for h in (h_hi, h_lo))
                    pe.matmul(o, wl, hh, start=(f == 0), stop=False)
                    pe.matmul(o, wh, hl, start=False, stop=False)
                    mm = pe.matmul(o, wh, hh, start=False, stop=(f == FC - 1))
                mm.then_inc(down_done, 1)

            pe.wait_ge(wlo_done, 2)
            pe.wait_ge(x2_done, NT)
            for f in range(FC):
                up(0, 0, f, f < 2)
            for f in range(FC):
                down(0, 0, f)
            with pe.Fori(0, R // 2) as i:
                e = i * 2 + 1
                for j in range(2):
                    s = 1 - j
                    pe.wait_ge(wlo_done, e + j + 1)
                    for f in range(FC):
                        up(e + j, s, f)
                    for f in range(FC):
                        down(e + j, s, f)
            for b in range(B):
                pe.wait_ge(acc_done, B * (NE - 1) + b + 1)
                for t in range(T):
                    mm = pe.transpose(bank(b)[:, t * P:(t + 1) * P], acc[:, b, t * P:(t + 1) * P], ident[:])
                mm.then_inc(back_done, 1)


_OUT = (2, 512, 128)


def kernel(**inputs):
    import numpy as np
    import concourse.bacc as bacc
    from concourse.bass_utils import run_bass_kernel_spmd

    a = {k: np.asarray(v) for k, v in inputs.items()}
    n = "L0_xattn_"
    m = "L0_ffn_"
    x, ctx = a["x"], a["ctx_1024"]
    batches, keys, width = ctx.shape
    w1 = np.concatenate([a[m + "shared_w1"][None], a[m + "spec_w1"]])
    w2 = np.concatenate([a[m + "shared_w2"][None], a[m + "spec_w2"]])
    b1 = np.concatenate([a[m + "shared_b1"][None], a[m + "spec_b1"]])
    b2 = np.concatenate([a[m + "shared_b2"][None], a[m + "spec_b2"]])
    experts, hidden, _ = w1.shape
    chunks = hidden // width
    w1t = w1.transpose(0, 2, 1)
    w2t = w2.transpose(0, 2, 1).reshape(experts, chunks, width, width).transpose(0, 2, 1, 3)
    arrays = {
        "x": x,
        "params": np.concatenate([
            a[n + "Wk"].T, a[n + "Wv"].T, a[n + "Wq"], a[n + "Wo"].T, ctx.reshape(batches * keys, width).T,
            a[n + "bq"][:, None], a[n + "bk"][:, None], a[n + "bv"][:, None], a[m + "router_w"].T,
            b1.reshape(experts * chunks, width).T, b2.T], axis=1),
        "rows": np.concatenate([a[n + "bo"], a[m + "router_b"]]),
        "mask": a["mask_BxS2_ik0"].reshape(1, batches * keys),
        "experts": np.concatenate([w1t, w2t.reshape(experts, width, hidden)], axis=2),
    }
    arrays["rows"] = arrays["rows"].reshape(1, -1)
    nc = bacc.Bacc("TRN2", target_bir_lowering=False, num_devices=1)
    feeds, args = {}, []
    for name, value in arrays.items():
        value = np.ascontiguousarray(value)
        feeds[f"in_{name}"] = value
        args.append(nc.dram_tensor(f"in_{name}", value.shape, mybir.dt.from_np(value.dtype),
                                   kind="ExternalInput").ap())
    args.append(nc.dram_tensor("out", _OUT, F32, kind="ExternalOutput").ap())
    xattn_moe_kernel(nc, *args)
    r = run_bass_kernel_spmd(nc, [feeds], core_ids=[0])
    return r.results[0]["out"]
```

```python
from contextlib import ExitStack

import concourse.bass as bass
from concourse import mybir

ALU = mybir.AluOpType
ACT = mybir.ActivationFunctionType
F32 = mybir.dt.float32
F32R = mybir.dt.float32r
I32 = mybir.dt.int32
U32 = mybir.dt.uint32
AX_X = mybir.AxisListType.X

P = 128
HEADS, HD = 16, 8
NEG = -1e30
EPS = 1e-5

C_WK, C_WV, C_WQ, C_WO = 0, P, 2 * P, 3 * P
C_CTX = 4 * P
HALF = 3


def xattn_moe_kernel(nc, x, params, rows, mask, experts, out):
    B, S, D = x.shape
    KEYS = mask.shape[1] // B
    HK = HEADS * KEYS
    T = S // P
    NT = B * T
    NE = experts.shape[0]
    R = NE - 1
    F = experts.shape[2] // 2
    FC = F // P
    HC = HK // P
    HG = P // KEYS
    VC = HG * (HD + 1)
    SCALE = float(HD) ** -0.5
    C_CTX4 = C_CTX + B * KEYS
    C_BQ = C_CTX4 + B * P
    C_BK = C_BQ + 1
    C_WR = C_BQ + 2
    C_B1 = C_WR + R
    C_B2 = C_B1 + NE * FC
    R_BO, R_BR, R_BV = 0, P, P + R
    LAST = NE - 1
    assert params.shape[1] == C_B2 + NE and S == 512 and D == P and HK == 512
    assert B == 2 and HALF % 2 == 1 and (LAST - HALF - 1) % 2 == 0

    combt_dram = nc.dram_tensor("combt_scratch", [R, B, S], F32, kind="Internal").ap()

    def slot(e):
        return e % 2 if e else 2

    with ExitStack() as ctx:
        def sb(name, shape, dt=F32):
            return ctx.enter_context(nc.sbuf_tensor(name, shape, dt))

        def sem(name):
            return ctx.enter_context(nc.semaphore(name))

        par = sb("par", [P, C_B2 + NE])
        rowb = sb("rowb", [P, rows.shape[1]])
        maskb = sb("maskb", [P, B * KEYS], I32)
        ident = sb("ident", [P, P])
        headmask = sb("headmask", [P, HEADS, KEYS])
        groupmask = sb("groupmask", [P, HG])
        iota8 = sb("iota8", [P, R])
        neghalf = sb("neghalf", [P, T])
        xin = sb("xin", [P, B, T, P])
        xb = sb("xb", [P, B, T, P])
        x2 = sb("x2", [P, B, T, P])
        xn = sb("xn", [P, B, T, P])
        stats = sb("stats", [P, T, 6])
        mv = sb("mv", [P, 2, B, T, 2])
        vareps = sb("vareps", [P, 2, B, T])
        rstd = sb("rstd", [P, 2, B, T])
        xt0 = sb("xt0", [P, B, T * P])
        q_hi = sb("q_hi", [P, B, T * P], F32R)
        q_lo = sb("q_lo", [P, B, T * P], F32R)
        k_full = sb("k_full", [P, B * KEYS])
        k_hi = sb("k_hi", [P, B * KEYS])
        k_lo = sb("k_lo", [P, B * KEYS])
        kbd_hi = sb("kbd_hi", [P, B, HEADS, KEYS], F32R)
        kbd_lo = sb("kbd_lo", [P, B, HEADS, KEYS], F32R)
        vb = sb("vb", [P, B, P])
        groupany = sb("groupany", [P, B, HG])
        vaug = sb("vaug", [P, B, HC, HG, HD + 1])
        isvalid = sb("isvalid", [P, B * KEYS])
        anyvalid = sb("anyvalid", [P, B])
        maskrow = sb("maskrow", [1, B, HK], F32R)
        ones_r = sb("ones_r", [1, P], F32R)
        rowmax = sb("rowmax", [P, 2, HEADS])
        probs = sb("probs", [P, T, HK])
        probt = sb("probt", [P, 2, HK])
        rrow = sb("rrow", [P, 2, HEADS])
        on = sb("on", [P, 2, P])
        ont = sb("ont", [P, 2, P])
        xt_hi = sb("xt_hi", [P, B, T * P], F32R)
        xt_lo = sb("xt_lo", [P, B, T * P], F32R)
        wr2 = sb("wr2", [P, 2 * R], F32R)
        loghi = sb("loghi", [P, B, T, R])
        logits = sb("logits", [P, B, T, R])
        top8 = sb("top8", [P, B, T, 8])
        idx8 = sb("idx8", [P, B, T, 8], U32)
        idxf = sb("idxf", [P, B, T, 2])
        gap = sb("gap", [P, B, T])
        w12 = sb("w12", [P, B, T, 2])
        tanhgap = sb("tanhgap", [P, B, T])
        hot = sb("hot", [P, B, T, 2, R])
        hotw = sb("hotw", [P, B, T, 2, R])
        comb = sb("comb", [P, B, T, R])
        combt = sb("combt", [R, B, T * P])
        combb = sb("combb", [P, 2, B, S])
        wst = sb("wst", [P, 3, 2 * F])
        w_hi = [sb(f"w_hi{s}", [P, 2 * F], F32R) for s in range(3)]
        w_lo = [sb(f"w_lo{s}", [P, 2 * F], F32R) for s in range(3)]
        b1cur = sb("b1cur", [P, 2, FC])
        h_full = sb("h_full", [P, FC, B * S])
        h_hi = sb("h_hi", [P, FC, B * S], F32R)
        h_lo = sb("h_lo", [P, FC, B * S], F32R)
        scaled = sb("scaled", [P, B, S])
        acc = sb("acc", [P, B, S])
        fin = sb("fin", [P, B, T, P])

        ps = [ctx.enter_context(nc.psum_tensor(f"ps{i}", [P, 1024], F32)) for i in range(4)]

        def bank(i):
            return ps[i // 2][:, 512 * (i % 2):512 * (i % 2) + 512]

        QB = (1, 2)
        SB = (3, 4)
        TB = 5
        MB = (6, 7)
        O_, OT_, Y_ = slice(0, HC * VC), slice(256, 384), slice(384, 512)
        DB = (2, 2, 2, 4, 5, 4)

        params_in, biases_in, rows_in, mask_in = (
            sem("params_in"), sem("biases_in"), sem("rows_in"), sem("mask_in"))
        x_in = [sem(f"x_in{b}") for b in range(B)]
        ident_ready, headmask_ready, groupmask_ready, neghalf_ready, iota_ready, ones_ready = (
            sem("ident_ready"), sem("headmask_ready"), sem("groupmask_ready"), sem("neghalf_ready"),
            sem("iota_ready"), sem("ones_ready"))
        xb_ready = sem("xb_ready")
        k_psum, v_psum, k_ready, khi_ready, klo_ready, kbd_ready = (
            sem("k_psum"), sem("v_psum"), sem("k_ready"), sem("khi_ready"), sem("klo_ready"), sem("kbd_ready"))
        valid_ready, any_ready, maskrow_ready = sem("valid_ready"), sem("any_ready"), sem("maskrow_ready")
        groupany_ready, vb_ready, vaug_ready = sem("groupany_ready"), sem("vb_ready"), sem("vaug_ready")
        wr_hi_ready, wr_ready = sem("wr_hi_ready"), sem("wr_ready")
        st_done = [sem(f"ln{k}_stats") for k in range(2)]
        mv_done = [sem(f"ln{k}_meanvar") for k in range(2)]
        ve_done = [sem(f"ln{k}_vareps") for k in range(2)]
        rs_done = [sem(f"ln{k}_rstd") for k in range(2)]
        xn_done = [sem(f"ln{k}_normed") for k in range(2)]
        tr_done = [sem(f"ln{k}_transposed") for k in range(2)]
        xt0_done, q_psum, qhi_done, qlo_done = sem("xt0_done"), sem("q_psum"), sem("qhi_done"), sem("qlo_done")
        xhi_done, xlo_done = sem("xhi_done"), sem("xlo_done")
        scores_done, max_done, shift_done, exp_done = (
            sem("scores_done"), sem("max_done"), sem("shift_done"), sem("exp_done"))
        ptr_done, probt_done, o_done, recip_done, on_done, ot_done, ont_done, y_done, x2_done = (
            sem("ptr_done"), sem("probt_done"), sem("o_done"), sem("recip_done"), sem("on_done"),
            sem("ot_done"), sem("ont_done"), sem("y_done"), sem("x2_done"))
        logit_psum, loghi_ready, logit_ready, top_ready, idx_ready, idxf_ready = (
            sem("logit_psum"), sem("loghi_ready"), sem("logit_ready"), sem("top_ready"), sem("idx_ready"),
            sem("idxf_ready"))
        gap_ready, tanh_ready, w12_ready = sem("gap_ready"), sem("tanh_ready"), sem("w12_ready")
        hot_ready, hotw_ready, comb_ready = sem("hot_ready"), sem("hotw_ready"), sem("comb_ready")
        combt_psum, combt_ready = sem("combt_psum"), sem("combt_ready")
        combt_stored = [sem(f"combt_stored{b}") for b in range(B)]
        half_comb_in = {(e, b): sem(f"half_comb_in{e}_{b}") for e in range(1, HALF) for b in range(B)}
        comb_in = [sem(f"comb_in{s}") for s in range(2)]
        w_in = [sem(f"w_in{s}") for s in range(3)]
        whi_done = [sem(f"w{n + 1}hi_done") for n in range(2)]
        wlo_done = [sem(f"w{n + 1}lo_done") for n in range(2)]
        b1_ready = sem("b1_ready")
        up_done, gelu_done, hhi_done, hlo_done, down_done = (
            sem("up_done"), sem("gelu_done"), sem("hhi_done"), sem("hlo_done"), sem("down_done"))
        acc_init, scaled_done, acc_done = sem("acc_init"), sem("scaled_done"), sem("acc_done")
        back_done, fin_done, out_stored = sem("back_done"), sem("fin_done"), sem("out_stored")

        def unit(e):
            return e + HALF

        def scaled_after(e, b):
            return 2 * (HALF - 1) + 2 * (e - HALF) + b + 1

        HALVES = [(e, b) for b in range(B) for e in range(HALF)]
        SCALED = {(e, b): b * (HALF - 1) + e for e, b in HALVES}

        block = ctx.enter_context(nc.Block())

        @block.sync
        def _(sp):
            sp.dma_start(xin[:, 0], x[0].rearrange("(p t) d -> p t d", t=T)).then_inc(x_in[0], 16)
            sp.dma_start(xin[:, 1], x[1].rearrange("(p t) d -> p t d", t=T)).then_inc(x_in[1], 16)

            def load_weights(e, s):
                sp.dma_start(wst[:, s], experts[e]).then_inc(w_in[s], 16)

            def load_comb(e, s):
                sp.dma_start(combb[:, s], combt_dram[e - 1].partition_broadcast(P)).then_inc(comb_in[s], 16)

            for e in range(HALF):
                load_weights(e, slot(e))
            sp.dma_start(par[:, C_B1:C_B2 + NE], params[:, C_B1:C_B2 + NE]).then_inc(biases_in, 16)
            for b in range(B):
                sp.wait_ge(combt_ready, b + 1)
                sp.dma_start(combt_dram[:, b], combt[:, b]).then_inc(combt_stored[b], 16)
                sp.wait_ge(combt_stored[b], 16)
                for e in range(1, HALF):
                    sp.dma_start(combb[:, e % 2, b],
                                 combt_dram[e - 1, b:b + 1].partition_broadcast(P)).then_inc(half_comb_in[e, b], 16)
            for e in (HALF, HALF + 1):
                sp.wait_ge(wlo_done[1], e - 1)
                sp.wait_ge(down_done, FC * (e - 1))
                load_weights(e, e % 2)
            sp.wait_ge(scaled_done, SCALED[HALF - 2, 1])
            load_comb(HALF, 1)
            with sp.Fori(0, (LAST - HALF - 1) // 2) as i:
                e = i * 2 + HALF
                for j in range(2):
                    sp.wait_ge(wlo_done[1], e + j + 1)
                    load_weights(e + j + 2, 1 - j)
                    sp.wait_ge(scaled_done, scaled_after(e + j - 1, 1))
                    load_comb(e + j + 1, j)
            sp.wait_ge(scaled_done, scaled_after(LAST - 2, 1))
            load_comb(LAST, 0)
            for b in range(B):
                sp.wait_ge(fin_done, b + 1)
                sp.dma_start(out[b].rearrange("(p t) d -> p t d", t=T), fin[:, b]).then_inc(out_stored, 16)
            sp.wait_ge(out_stored, 16 * B)

        @block.gpsimd
        def _(pool):
            pool.memset(ident[:], 0.0).then_inc(ident_ready, 1)
            pool.memset(neghalf[:], -0.5).then_inc(neghalf_ready, 1)
            pool.memset(headmask[:], 1.0).then_inc(headmask_ready, 1)
            pool.memset(groupmask[:], 1.0).then_inc(groupmask_ready, 1)

            def keep(tile, ready, n, base, pattern, channel):
                pool.wait_ge(ready, n)
                pool.affine_select(out=tile, in_=tile, compare_op=ALU.is_ge, fill=0.0, base=base,
                                   pattern=pattern, channel_multiplier=channel).then_inc(ready, 1)

            pool.wait_ge(ident_ready, 1)
            pool.affine_select(out=ident[:], in_=ident[:], compare_op=ALU.not_equal, fill=1.0, base=0,
                               pattern=[[-1, P]], channel_multiplier=1).then_inc(ident_ready, 1)
            keep(headmask[:], headmask_ready, 1, 0, [[-HD, HEADS], [0, KEYS]], 1)
            keep(headmask[:], headmask_ready, 2, HD - 1, [[HD, HEADS], [0, KEYS]], -1)
            keep(groupmask[:], groupmask_ready, 1, 0, [[-KEYS, HG]], 1)
            keep(groupmask[:], groupmask_ready, 2, KEYS - 1, [[KEYS, HG]], -1)
            pool.iota(iota8[:], pattern=[[1, R]], base=0, channel_multiplier=0,
                      allow_small_or_imprecise_dtypes=True).then_inc(iota_ready, 1)

            def rstd_of(k, b):
                pool.wait_ge(ve_done[k], b + 1)
                pool.tensor_tensor(rstd[:, k, b], vareps[:, k, b], neghalf[:], ALU.pow).then_inc(rs_done[k], 1)

            def block_k(b):
                for part, source in ((kbd_hi, k_hi), (kbd_lo, k_lo)):
                    pool.tensor_tensor(part[:, b], headmask[:],
                                       source[:, b * KEYS:(b + 1) * KEYS].unsqueeze(1)
                                       .broadcast_to([P, HEADS, KEYS]), ALU.mult).then_inc(kbd_ready, 1)

            def mask_row(b):
                pool.tensor_scalar(maskrow[:, b].rearrange("p (h k) -> p h k", h=HEADS),
                                   isvalid[0:1, b * KEYS:(b + 1) * KEYS].unsqueeze(1)
                                   .broadcast_to([1, HEADS, KEYS]),
                                   -NEG, NEG, ALU.mult, ALU.add).then_inc(maskrow_ready, 1)

            def add_bo(b):
                pool.wait_ge(rows_in, 16)
                pool.wait_ge(x_in[b], 16)
                pool.tensor_tensor(xb[:, b], xin[:, b],
                                   rowb[:, R_BO:R_BO + P].unsqueeze(1).broadcast_to([P, T, P]),
                                   ALU.add).then_inc(xb_ready, 1)

            def split_w_lo(e, s, n):
                part = slice(n * F, (n + 1) * F)
                pool.wait_ge(whi_done[n], e + 1)
                pool.tensor_tensor(w_lo[s][:, part], wst[:, s, part], w_hi[s][:, part].bitcast(F32),
                                   ALU.subtract).then_inc(wlo_done[n], 1)

            def accumulate(b, n, before):
                pool.wait_ge(scaled_done, n)
                if before is not None:
                    pool.wait_ge(acc_done, before)
                pool.tensor_tensor(acc[:, b], acc[:, b], scaled[:, b], ALU.add).then_inc(acc_done, 1)

            pool.wait_ge(neghalf_ready, 1)
            rstd_of(0, 0)
            pool.wait_ge(headmask_ready, 3)
            pool.wait_ge(klo_ready, 1)
            block_k(0)
            rstd_of(0, 1)
            pool.wait_ge(valid_ready, 1)
            mask_row(0)
            block_k(1)
            mask_row(1)
            add_bo(0)
            split_w_lo(0, slot(0), 0)
            add_bo(1)
            split_w_lo(1, slot(1), 0)
            rstd_of(1, 0)
            split_w_lo(2, slot(2), 0)
            rstd_of(1, 1)
            for e in range(HALF):
                split_w_lo(e, slot(e), 1)
            for e, b in HALVES:
                if e == 1:
                    pool.wait_ge(acc_init, b + 1)
                if e:
                    accumulate(b, SCALED[e, b], SCALED[e, b] - 1 if e > 1 else None)
                if (e, b) == (HALF - 2, B - 1):
                    split_w_lo(HALF, 1, 0)
                    split_w_lo(HALF + 1, 0, 0)
                    split_w_lo(HALF, 1, 1)
            with pool.Fori(0, (LAST - HALF - 1) // 2) as i:
                e = i * 2 + HALF
                for j in range(2):
                    split_w_lo(e + j + 2, 1 - j, 0)
                    split_w_lo(e + j + 1, j, 1)
                    for b in range(B):
                        accumulate(b, scaled_after(e + j, b), scaled_after(e + j - 1, b))
            split_w_lo(LAST, 0, 1)
            for e in (LAST - 1, LAST):
                for b in range(B):
                    accumulate(b, scaled_after(e, b), scaled_after(e - 1, b))

        @block.scalar
        def _(act):
            act.dma_start(par[:, 0:C_B1], params[:, 0:C_B1]).then_inc(params_in, 16)
            act.dma_start(rowb[:], rows.partition_broadcast(P)).then_inc(rows_in, 16)
            act.dma_start(maskb[:], mask.partition_broadcast(P)).then_inc(mask_in, 16)

            def copy_xt0(b):
                act.wait_ge(tr_done[0], b + 1)
                act.activation(xt0[:, b], bank(TB), ACT.Copy).then_inc(xt0_done, 1)

            def q_high(b):
                act.wait_ge(q_psum, b + 1)
                act.activation(q_hi[:, b], bank(QB[b]), ACT.Identity,
                               bias=par[:, C_BQ:C_BQ + 1]).then_inc(qhi_done, 1)

            def exp(i):
                act.wait_ge(shift_done, i + 1)
                act.activation(probs[:, i % T], probs[:, i % T], ACT.Exp).then_inc(exp_done, 1)

            def copy_probt(i):
                act.wait_ge(ptr_done, i + 1)
                if i >= 2:
                    act.wait_ge(o_done, i - 1)
                act.activation(probt[:, i % 2], bank(TB), ACT.Copy).then_inc(probt_done, 1)

            def copy_ont(i):
                act.wait_ge(ot_done, i + 1)
                if i >= 2:
                    act.wait_ge(y_done, i - 1)
                act.activation(ont[:, i % 2], bank(MB[i % 2])[:, OT_], ACT.Copy).then_inc(ont_done, 1)

            def xt_high(b):
                act.wait_ge(tr_done[1], b + 1)
                act.activation(xt_hi[:, b], bank(TB), ACT.Copy).then_inc(xhi_done, 1)

            def router_tanh(b):
                act.wait_ge(gap_ready, b + 1)
                act.activation(tanhgap[:, b], gap[:, b], ACT.Tanh, scale=0.5).then_inc(tanh_ready, 1)

            def copy_combt(b):
                act.wait_ge(combt_psum, b + 1)
                act.activation(combt[:, b], bank(TB)[0:R], ACT.Copy).then_inc(combt_ready, 1)

            def gelu_half(u, f):
                e, b = HALVES[u]
                src = bank(f % 2)
                b1 = par[:, C_B1 + e * FC + f:C_B1 + e * FC + f + 1]
                dst = slice(b * S, (b + 1) * S)
                act.wait_ge(up_done, FC * u + f + 1)
                if 0 < u < HALF:
                    act.wait_ge(down_done, FC * (u - 1) + f + 1)
                if u > HALF:
                    act.wait_ge(hlo_done, FC * (u - 1 - HALF) + f + 1)
                act.activation(h_full[:, f, dst], src, ACT.Gelu_apprx_tanh, bias=b1).then_inc(gelu_done, 1)
                if u >= HALF:
                    if u > HALF:
                        act.wait_ge(down_done, FC * (u - 1) + f + 1)
                    act.activation(h_hi[:, f, dst], src, ACT.Gelu_apprx_tanh, bias=b1).then_inc(hhi_done, 1)

            def take_b1(e, s):
                act.activation(b1cur[:, s], par[:, bass.ds(C_B1 + e * FC, FC)], ACT.Copy).then_inc(b1_ready, 1)

            def gelu(e, s, f):
                src = ps[f % 2][:]
                b1 = b1cur[:, s, f:f + 1]
                act.wait_ge(b1_ready, e - HALF + 1)
                act.wait_ge(up_done, FC * unit(e) + f + 1)
                act.wait_ge(hlo_done, FC * (e - 1) + f + 1)
                act.activation(h_full[:, f], src, ACT.Gelu_apprx_tanh, bias=b1).then_inc(gelu_done, 1)
                act.wait_ge(down_done, FC * (unit(e) - 1) + f + 1)
                act.activation(h_hi[:, f], src, ACT.Gelu_apprx_tanh, bias=b1).then_inc(hhi_done, 1)

            copy_xt0(0)
            q_high(0)
            copy_xt0(1)
            for s in range(NT + 3):
                if s >= 3:
                    copy_ont(s - 3)
                if 1 <= s <= NT:
                    copy_probt(s - 1)
                if s < NT:
                    exp(s)
                if s == 1:
                    q_high(1)
                if s == T + 4:
                    xt_high(0)
                    act.wait_ge(biases_in, 16)
            for u in range(2 * HALF):
                for f in range(FC):
                    gelu_half(u, f)
                    if (u, f) == (0, 1):
                        router_tanh(0)
                    if (u, f) == (0, 3):
                        copy_combt(0)
                    if (u, f) == (1, 3):
                        xt_high(1)
                    if (u, f) == (2, 1):
                        router_tanh(1)
                    if (u, f) == (3, 1):
                        copy_combt(1)
            take_b1(HALF, 1)
            for f in range(FC):
                gelu(HALF, 1, f)
            take_b1(HALF + 1, 0)
            with act.Fori(0, (LAST - HALF - 1) // 2) as i:
                e = i * 2 + HALF
                for j in range(2):
                    for f in range(FC):
                        gelu(e + j + 1, j, f)
                    take_b1(e + j + 2, 1 - j)
            for f in range(FC):
                gelu(LAST, 0, f)

        @block.vector
        def _(dve):
            dve.memset(ones_r[:].bitcast(F32), 1.0).then_inc(ones_ready, 1)

            def meanvar(k, b, src):
                for t in range(T):
                    dve.bn_stats(stats[:, t], src[:, b, t]).then_inc(st_done[k], 1)
                for t in range(T):
                    dve.wait_ge(st_done[k], T * b + t + 1)
                    dve.bn_aggr(mv[:, k, b, t], stats[:, t]).then_inc(mv_done[k], 1)
                dve.wait_ge(mv_done[k], T * (b + 1))
                dve.tensor_scalar(vareps[:, k, b], mv[:, k, b, :, 1], EPS, None, ALU.add).then_inc(ve_done[k], 1)

            def norm(k, b, src):
                dve.wait_ge(rs_done[k], b + 1)
                for t in range(T):
                    dve.tensor_scalar(xn[:, b, t], src[:, b, t], mv[:, k, b, t, 0:1], rstd[:, k, b, t:t + 1],
                                      ALU.subtract, ALU.mult).then_inc(xn_done[k], 1)

            def heads(ap):
                return ap.rearrange("p (h k) -> p h k", h=HEADS)

            def q_low(b):
                dve.wait_ge(qhi_done, b + 1)
                dve.scalar_tensor_tensor(out=q_lo[:, b], in0=bank(QB[b]), scalar=par[:, C_BQ:C_BQ + 1],
                                         in1=q_hi[:, b].bitcast(F32), op0=ALU.add,
                                         op1=ALU.subtract).then_inc(qlo_done, 1)

            def shift(i):
                sc = heads(bank(SB[i % 2]))
                dve.wait_ge(scores_done, i + 1)
                dve.tensor_reduce(rowmax[:, i % 2], sc, AX_X, ALU.max).then_inc(max_done, 1)
                dve.wait_ge(max_done, i + 1)
                if i >= T:
                    dve.wait_ge(ptr_done, i - T + 1)
                dve.tensor_tensor(heads(probs[:, i % T]), sc,
                                  rowmax[:, i % 2].unsqueeze(2).broadcast_to([P, HEADS, KEYS]),
                                  ALU.subtract).then_inc(shift_done, 1)

            def normalise(i):
                o = bank(MB[i % 2])[:, O_].rearrange("p (h c) -> p h c", h=HEADS)
                dve.wait_ge(o_done, i + 1)
                dve.reciprocal(rrow[:, i % 2], o[:, :, HD]).then_inc(recip_done, 1)
                dve.wait_ge(recip_done, i + 1)
                if i >= 2:
                    dve.wait_ge(ot_done, i - 1)
                dve.tensor_tensor(on[:, i % 2].rearrange("p (h d) -> p h d", h=HEADS), o[:, :, 0:HD],
                                  rrow[:, i % 2].unsqueeze(2).broadcast_to([P, HEADS, HD]),
                                  ALU.mult).then_inc(on_done, 1)

            def residual(i):
                dve.wait_ge(y_done, i + 1)
                dve.wait_ge(xb_ready, i // T + 1)
                dve.tensor_tensor(x2[:, i // T, i % T], bank(MB[i % 2])[:, Y_], xb[:, i // T, i % T],
                                  ALU.add).then_inc(x2_done, 1)

            def xt_low(b):
                dve.wait_ge(xhi_done, b + 1)
                dve.tensor_tensor(xt_lo[:, b], bank(TB), xt_hi[:, b].bitcast(F32),
                                  ALU.subtract).then_inc(xlo_done, 1)

            def split_w_hi(e, s, n):
                part = slice(n * F, (n + 1) * F)
                if isinstance(e, int) and e < HALF:
                    dve.wait_ge(w_in[s], 16)
                else:
                    dve.wait_ge(w_in[s], e * 8 + (8 if s == 1 else 0))
                    dve.wait_ge((up_done, down_done)[n], FC * (e + 2))
                dve.tensor_copy(w_hi[s][:, part], wst[:, s, part]).then_inc(whi_done[n], 1)

            def route_top(b):
                dve.wait_ge(logit_psum, b + 1)
                lg = bank(TB)[:, 0:2 * T * R].rearrange("p (t e) -> p t e", t=T)
                dve.tensor_tensor(loghi[:, b], lg[:, :, 0:R],
                                  rowb[:, R_BR:R_BR + R].unsqueeze(1).broadcast_to([P, T, R]),
                                  ALU.add).then_inc(loghi_ready, 1)
                dve.wait_ge(loghi_ready, b + 1)
                dve.tensor_tensor(logits[:, b], lg[:, :, R:2 * R], loghi[:, b], ALU.add).then_inc(logit_ready, 1)
                dve.wait_ge(logit_ready, b + 1)
                for t in range(T):
                    dve.max(top8[:, b, t], logits[:, b, t]).then_inc(top_ready, 1)
                dve.wait_ge(top_ready, T * (b + 1))
                dve.tensor_tensor(gap[:, b], top8[:, b, :, 1], top8[:, b, :, 0], ALU.subtract).then_inc(gap_ready, 1)
                for t in range(T):
                    dve.max_index(idx8[:, b, t], top8[:, b, t], logits[:, b, t]).then_inc(idx_ready, 1)

            def route_weights(b):
                dve.wait_ge(idx_ready, T * (b + 1))
                dve.tensor_copy(idxf[:, b], idx8[:, b, :, 0:2]).then_inc(idxf_ready, 1)
                dve.wait_ge(tanh_ready, b + 1)
                for n, sign in enumerate((-0.5, 0.5)):
                    dve.tensor_scalar(w12[:, b, :, n], tanhgap[:, b], sign, 0.5, ALU.mult,
                                      ALU.add).then_inc(w12_ready, 1)
                dve.wait_ge(idxf_ready, b + 1)
                dve.tensor_tensor(hot[:, b],
                                  iota8[:].unsqueeze(1).unsqueeze(1).broadcast_to([P, T, 2, R]),
                                  idxf[:, b].unsqueeze(3).broadcast_to([P, T, 2, R]),
                                  ALU.is_equal).then_inc(hot_ready, 1)
                dve.wait_ge(w12_ready, 2 * (b + 1))
                dve.wait_ge(hot_ready, b + 1)
                dve.tensor_tensor(hotw[:, b], hot[:, b], w12[:, b].unsqueeze(3).broadcast_to([P, T, 2, R]),
                                  ALU.mult).then_inc(hotw_ready, 1)
                dve.wait_ge(hotw_ready, b + 1)
                dve.tensor_tensor(comb[:, b], hotw[:, b, :, 0], hotw[:, b, :, 1], ALU.add).then_inc(comb_ready, 1)

            dve.wait_ge(x_in[0], 16)
            meanvar(0, 0, xin)
            dve.wait_ge(k_psum, 1)
            dve.tensor_scalar(k_full[:], bank(MB[1])[:, 0:B * KEYS], par[:, C_BK:C_BK + 1], SCALE,
                              ALU.add, ALU.mult).then_inc(k_ready, 1)
            dve.wait_ge(k_ready, 1)
            dve.tensor_copy(k_hi[:].bitcast(F32R), k_full[:]).then_inc(khi_ready, 1)
            dve.wait_ge(khi_ready, 1)
            dve.tensor_tensor(k_lo[:], k_full[:], k_hi[:], ALU.subtract).then_inc(klo_ready, 1)
            norm(0, 0, xin)
            dve.wait_ge(x_in[1], 16)
            meanvar(0, 1, xin)
            dve.wait_ge(mask_in, 16)
            dve.tensor_scalar(isvalid[:], maskb[:], 0.0, None, ALU.not_equal).then_inc(valid_ready, 1)
            dve.wait_ge(valid_ready, 1)
            dve.tensor_reduce(anyvalid[:], isvalid[:].rearrange("p (b k) -> p b k", b=B), AX_X,
                              ALU.max).then_inc(any_ready, 1)
            split_w_hi(0, slot(0), 0)
            norm(0, 1, xin)
            dve.wait_ge(v_psum, 1)
            dve.wait_ge(rows_in, 16)
            for b in range(B):
                dve.tensor_tensor(vb[:, b], bank(MB[0])[:, b * P:(b + 1) * P], rowb[:, R_BV:R_BV + P],
                                  ALU.add).then_inc(vb_ready, 1)
            dve.wait_ge(groupmask_ready, 3)
            dve.wait_ge(any_ready, 1)
            for b in range(B):
                dve.tensor_scalar(groupany[:, b], groupmask[:], anyvalid[:, b:b + 1], None,
                                  ALU.mult).then_inc(groupany_ready, 1)
            for b in range(B):
                dve.tensor_copy(vaug[:, b, :, :, HD],
                                groupmask[:].unsqueeze(1).broadcast_to([P, HC, HG])).then_inc(vaug_ready, 1)
            dve.wait_ge(vb_ready, B)
            dve.wait_ge(groupany_ready, B)
            for b in range(B):
                for c in range(HC):
                    dve.tensor_tensor(vaug[:, b, c, :, 0:HD],
                                      vb[:, b, c * HG * HD:(c + 1) * HG * HD].rearrange("p (h d) -> p h d", h=HG),
                                      groupany[:, b].unsqueeze(2).broadcast_to([P, HG, HD]),
                                      ALU.mult).then_inc(vaug_ready, 1)
            q_low(0)
            dve.tensor_copy(wr2[:, 0:R], par[:, C_WR:C_WR + R]).then_inc(wr_hi_ready, 1)
            dve.wait_ge(wr_hi_ready, 1)
            dve.tensor_tensor(wr2[:, R:2 * R], par[:, C_WR:C_WR + R], wr2[:, 0:R].bitcast(F32),
                              ALU.subtract).then_inc(wr_ready, 1)

            def attention_step(s):
                if s < NT:
                    shift(s)
                if 2 <= s < NT + 2:
                    normalise(s - 2)
                if 3 <= s < NT + 3:
                    residual(s - 3)

            for s in range(T + 3):
                attention_step(s)
                if s == 1:
                    q_low(1)
                if s in (2, 3):
                    split_w_hi(s - 1, slot(s - 1), 0)
                if s > 3:
                    split_w_hi(s - 4, slot(s - 4), 1)
            dve.wait_ge(x2_done, T)
            meanvar(1, 0, x2)
            attention_step(T + 3)
            norm(1, 0, x2)
            attention_step(T + 4)
            xt_low(0)
            attention_step(T + 5)
            route_top(0)
            attention_step(T + 6)
            dve.wait_ge(x2_done, 2 * T)
            meanvar(1, 1, x2)
            route_weights(0)
            norm(1, 1, x2)
            dve.wait_ge(biases_in, 16)

            def start_sum(b, u):
                dve.wait_ge(down_done, FC * (u + 1))
                dve.tensor_scalar(acc[:, b], bank(DB[u]), par[:, C_B2:C_B2 + 1], None,
                                  ALU.add).then_inc(acc_init, 1)

            def weigh_half(u):
                e, b = HALVES[u]
                dve.wait_ge(down_done, FC * (u + 1))
                dve.wait_ge(half_comb_in[e, b], 16)
                if e > 1:
                    dve.wait_ge(acc_done, SCALED[e, b] - 1)
                dve.scalar_tensor_tensor(out=scaled[:, b], in0=bank(DB[u]), scalar=par[:, C_B2 + e:C_B2 + e + 1],
                                         in1=combb[:, e % 2, b], op0=ALU.add, op1=ALU.mult).then_inc(scaled_done, 1)

            def h_low_half(u, f):
                dst = slice(HALVES[u][1] * S, (HALVES[u][1] + 1) * S)
                dve.wait_ge(gelu_done, FC * u + f + 1)
                dve.wait_ge(hhi_done, FC * (u - HALF) + f + 1)
                dve.tensor_tensor(h_lo[:, f, dst], h_full[:, f, dst], h_hi[:, f, dst].bitcast(F32),
                                  ALU.subtract).then_inc(hlo_done, 1)

            start_sum(0, 0)
            xt_low(1)
            route_top(1)
            weigh_half(1)
            route_weights(1)
            for u in range(HALF, 2 * HALF):
                for f in range(FC):
                    h_low_half(u, f)
                if HALVES[u - 1][0]:
                    weigh_half(u - 1)
                else:
                    start_sum(1, u - 1)
            split_w_hi(HALF, 1, 0)

            def h_low(e, f):
                dve.wait_ge(gelu_done, FC * unit(e) + f + 1)
                dve.wait_ge(hhi_done, FC * e + f + 1)
                dve.tensor_tensor(h_lo[:, f], h_full[:, f], h_hi[:, f].bitcast(F32),
                                  ALU.subtract).then_inc(hlo_done, 1)

            def weigh(e, s):
                b2 = par[:, bass.ds(C_B2 + e, 1)]
                dve.wait_ge(down_done, FC * (unit(e) + 1))
                dve.wait_ge(comb_in[s], e * 8 - (8 if s == 1 else 16))
                for b in range(B):
                    dve.wait_ge(acc_done, scaled_after(e - 1, b))
                    dve.scalar_tensor_tensor(out=scaled[:, b], in0=ps[2 + s][:, b * S:(b + 1) * S], scalar=b2,
                                             in1=combb[:, s, b], op0=ALU.add, op1=ALU.mult).then_inc(scaled_done, 1)

            split_w_hi(HALF + 1, 0, 0)
            split_w_hi(HALF, 1, 1)
            for f in range(FC):
                h_low(HALF, f)
            weigh_half(2 * HALF - 1)
            with dve.Fori(0, (LAST - HALF - 1) // 2) as i:
                e = i * 2 + HALF
                for j in range(2):
                    h_low(e + j + 1, 0)
                    split_w_hi(e + j + 2, 1 - j, 0)
                    split_w_hi(e + j + 1, j, 1)
                    for f in range(1, FC):
                        h_low(e + j + 1, f)
                    weigh(e + j, 1 - j)
            h_low(LAST, 0)
            split_w_hi(LAST, 0, 1)
            for f in range(1, FC):
                h_low(LAST, f)
            weigh(LAST - 1, 1)
            weigh(LAST, 0)
            for b in range(B):
                dve.wait_ge(back_done, b + 1)
                dve.tensor_tensor(fin[:, b].rearrange("p t d -> p (t d)"), bank(b),
                                  x2[:, b].rearrange("p t d -> p (t d)"), ALU.add).then_inc(fin_done, 1)

        @block.tensor
        def _(pe):
            def transpose_norm(k, b):
                if b == 0 and k == 1:
                    pe.wait_ge(probt_done, NT)
                for t in range(T):
                    pe.wait_ge(xn_done[k], T * b + t + 1)
                    mm = pe.transpose(bank(TB)[:, t * P:(t + 1) * P], xn[:, b, t], ident[:])
                mm.then_inc(tr_done[k], 1)

            def project_q(b):
                pe.wait_ge(xt0_done, b + 1)
                pe.matmul(bank(QB[b]), par[:, C_WQ:C_WQ + P], xt0[:, b], start=True, stop=True).then_inc(q_psum, 1)

            def scores(i):
                b, t = divmod(i, T)
                if t == 0:
                    pe.wait_ge(qlo_done, b + 1)
                    pe.wait_ge(kbd_ready, 2 * (b + 1))
                    pe.wait_ge(maskrow_ready, b + 1)
                if i >= 2:
                    pe.wait_ge(shift_done, i - 1)
                qh, ql = (a[:, b, t * P:(t + 1) * P] for a in (q_hi, q_lo))
                kh, kl = (a[:, b].rearrange("p h k -> p (h k)") for a in (kbd_hi, kbd_lo))
                o = bank(SB[i % 2])
                pe.matmul(o, ones_r[:], maskrow[:, b], start=True, stop=False)
                pe.matmul(o, qh, kl, start=False, stop=False)
                pe.matmul(o, ql, kh, start=False, stop=False)
                pe.matmul(o, qh, kh, start=False, stop=True).then_inc(scores_done, 1)

            def transpose_probs(i):
                pe.wait_ge(exp_done, i + 1)
                if i >= 1:
                    pe.wait_ge(probt_done, i)
                for c in range(HC):
                    mm = pe.transpose(bank(TB)[:, c * P:(c + 1) * P], probs[:, i % T, c * P:(c + 1) * P], ident[:])
                mm.then_inc(ptr_done, 1)

            def attend(i):
                pe.wait_ge(probt_done, i + 1)
                if i < 2:
                    pe.wait_ge(vaug_ready, B + B * HC)
                else:
                    pe.wait_ge(x2_done, i - 1)
                for c in range(HC):
                    mm = pe.matmul(bank(MB[i % 2])[:, c * VC:(c + 1) * VC], probt[:, i % 2, c * P:(c + 1) * P],
                                   vaug[:, i // T, c].rearrange("p h c -> p (h c)"), start=True, stop=True)
                mm.then_inc(o_done, 1)

            def transpose_on(i):
                pe.wait_ge(on_done, i + 1)
                pe.transpose(bank(MB[i % 2])[:, OT_], on[:, i % 2], ident[:]).then_inc(ot_done, 1)

            def project_out(i):
                pe.wait_ge(ont_done, i + 1)
                pe.matmul(bank(MB[i % 2])[:, Y_], ont[:, i % 2], par[:, C_WO:C_WO + P],
                          start=True, stop=True).then_inc(y_done, 1)

            def router(b):
                pe.wait_ge(xlo_done, b + 1)
                for t in range(T):
                    o = bank(TB)[:, t * 2 * R:(t + 1) * 2 * R]
                    pe.matmul(o, xt_lo[:, b, t * P:(t + 1) * P], wr2[:], start=True, stop=False)
                    mm = pe.matmul(o, xt_hi[:, b, t * P:(t + 1) * P], wr2[:], start=False, stop=True)
                mm.then_inc(logit_psum, 1)

            def transpose_comb(b):
                pe.wait_ge(comb_ready, b + 1)
                for t in range(T):
                    mm = pe.transpose(bank(TB)[0:R, t * P:(t + 1) * P], comb[:, b, t], ident[:])
                mm.then_inc(combt_psum, 1)

            def up_half(u, f):
                e, b = HALVES[u]
                if f == 0:
                    pe.wait_ge(wlo_done[0], e + 1)
                    pe.wait_ge(xlo_done, b + 1)
                n = FC * u + f - 1
                if n > 0 and n <= FC * HALF:
                    pe.wait_ge(gelu_done, n)
                elif n > 0:
                    pe.wait_ge(hhi_done, n - FC * HALF)
                wh, wl = (w[slot(e)][:, f * P:(f + 1) * P] for w in (w_hi, w_lo))
                pe.matmul(bank(f % 2), wl, xt_hi[:, b], start=True, stop=False)
                pe.matmul(bank(f % 2), wh, xt_lo[:, b], start=False, stop=False)
                pe.matmul(bank(f % 2), wh, xt_hi[:, b], start=False, stop=True).then_inc(up_done, 1)

            def down_half(u, f):
                e, b = HALVES[u]
                o = bank(DB[u])
                if f == 0:
                    if u == 1:
                        pe.wait_ge(acc_init, 1)
                    if u == 2:
                        pe.wait_ge(scaled_done, SCALED[HALVES[1]])
                    if u == 3:
                        pe.wait_ge(shift_done, NT)
                    if u == 4:
                        pe.wait_ge(combt_ready, B)
                    if u == 5:
                        pe.wait_ge(acc_init, B)
                w2 = slice(F + f * P, F + (f + 1) * P)
                dst = slice(b * S, (b + 1) * S)
                first, last = f == 0, f == FC - 1
                if u < HALF:
                    pe.wait_ge(gelu_done, FC * u + f + 1)
                    pe.matmul(o, wst[:, slot(e), w2], h_full[:, f, dst], start=first,
                              stop=last).then_inc(down_done, 1)
                else:
                    pe.wait_ge(wlo_done[1], e + 1)
                    pe.wait_ge(hlo_done, FC * (u - HALF) + f + 1)
                    pe.matmul(o, w_lo[slot(e)][:, w2], h_hi[:, f, dst], start=first, stop=False)
                    pe.matmul(o, w_hi[slot(e)][:, w2], h_lo[:, f, dst], start=False, stop=False)
                    pe.matmul(o, w_hi[slot(e)][:, w2], h_hi[:, f, dst], start=False,
                              stop=last).then_inc(down_done, 1)

            def up(e, s, f):
                if f == 0:
                    pe.wait_ge(wlo_done[0], e + 1)
                pe.wait_ge(hhi_done, FC * e + (f - 1))
                wh, wl = (w[s][:, f * P:(f + 1) * P] for w in (w_hi, w_lo))
                for b in range(B):
                    o = ps[f % 2][:, b * S:(b + 1) * S]
                    pe.matmul(o, wl, xt_hi[:, b], start=True, stop=False)
                    pe.matmul(o, wh, xt_lo[:, b], start=False, stop=False)
                    mm = pe.matmul(o, wh, xt_hi[:, b], start=False, stop=True)
                mm.then_inc(up_done, 1)

            def down(e, s, f):
                if f == 0:
                    pe.wait_ge(scaled_done, scaled_after(e - 2, 1))
                    pe.wait_ge(wlo_done[1], e + 1)
                pe.wait_ge(hlo_done, FC * e + f + 1)
                wh, wl = (w[s][:, F + f * P:F + (f + 1) * P] for w in (w_hi, w_lo))
                for b in range(B):
                    o = ps[2 + s][:, b * S:(b + 1) * S]
                    hh, hl = (h[:, f, b * S:(b + 1) * S] for h in (h_hi, h_lo))
                    pe.matmul(o, wl, hh, start=(f == 0), stop=False)
                    pe.matmul(o, wh, hl, start=False, stop=False)
                    mm = pe.matmul(o, wh, hh, start=False, stop=(f == FC - 1))
                mm.then_inc(down_done, 1)

            pe.wait_ge(params_in, 16)
            pe.matmul(bank(MB[1])[:, 0:B * KEYS], par[:, C_WK:C_WK + P],
                      par[:, C_CTX:C_CTX + B * KEYS], start=True, stop=True).then_inc(k_psum, 1)
            for b in range(B):
                mm = pe.matmul(bank(MB[0])[:, b * P:(b + 1) * P], par[:, C_CTX4 + b * P:C_CTX4 + (b + 1) * P],
                               par[:, C_WV:C_WV + P], start=True, stop=True)
            mm.then_inc(v_psum, 1)
            pe.wait_ge(ident_ready, 2)
            transpose_norm(0, 0)
            project_q(0)
            pe.wait_ge(xt0_done, 1)
            transpose_norm(0, 1)
            pe.wait_ge(ones_ready, 1)
            scores(0)
            project_q(1)
            pe.wait_ge(xt0_done, B)

            def attention_step(s):
                if s + 1 < NT:
                    scores(s + 1)
                if 3 <= s < NT + 3:
                    project_out(s - 3)
                if 1 <= s <= NT:
                    attend(s - 1)
                if 2 <= s < NT + 2:
                    transpose_on(s - 2)
                if s < NT:
                    transpose_probs(s)

            for s in range(T + 4):
                attention_step(s)
            transpose_norm(1, 0)
            attention_step(T + 4)
            up_half(0, 0)
            attention_step(T + 5)
            pe.wait_ge(wr_ready, 1)
            router(0)
            up_half(0, 1)
            attention_step(T + 6)
            up_half(0, 2)
            up_half(0, 3)
            for u in range(1, 2 * HALF):
                for f in range(FC):
                    if (u, f) == (1, 1):
                        transpose_comb(0)
                    if (u, f) == (1, 3):
                        pe.wait_ge(combt_ready, 1)
                        transpose_norm(1, 1)
                    if (u, f) == (2, 1):
                        router(1)
                    if (u, f) == (3, 1):
                        transpose_comb(1)
                    up_half(u, f)
                    down_half(u - 1, f)
            for f in range(FC):
                if f == 0:
                    pe.wait_ge(hhi_done, FC * HALF)
                up(HALF, 1, f)
                down_half(2 * HALF - 1, f)
            with pe.Fori(0, (LAST - HALF - 1) // 2) as i:
                e = i * 2 + HALF
                for j in range(2):
                    for f in range(FC):
                        up(e + j + 1, j, f)
                        down(e + j, 1 - j, f)
            for f in range(FC):
                up(LAST, 0, f)
                down(LAST - 1, 1, f)
            for f in range(FC):
                down(LAST, 0, f)
            for b in range(B):
                pe.wait_ge(acc_done, scaled_after(LAST, b))
                for t in range(T):
                    mm = pe.transpose(bank(b)[:, t * P:(t + 1) * P], acc[:, b, t * P:(t + 1) * P], ident[:])
                mm.then_inc(back_done, 1)


_OUT = (2, 512, 128)


def kernel(**inputs):
    import numpy as np
    import concourse.bacc as bacc
    from concourse.bass_utils import run_bass_kernel_spmd

    a = {k: np.asarray(v) for k, v in inputs.items()}
    n = "L0_xattn_"
    m = "L0_ffn_"
    x, ctx = a["x"], a["ctx_1024"]
    batches, keys, width = ctx.shape
    w1 = np.concatenate([a[m + "shared_w1"][None], a[m + "spec_w1"]])
    w2 = np.concatenate([a[m + "shared_w2"][None], a[m + "spec_w2"]])
    b1 = np.concatenate([a[m + "shared_b1"][None], a[m + "spec_b1"]])
    b2 = np.concatenate([a[m + "shared_b2"][None], a[m + "spec_b2"]])
    experts, hidden, _ = w1.shape
    chunks = hidden // width
    w1t = w1.transpose(0, 2, 1)
    w2t = w2.transpose(0, 2, 1).reshape(experts, chunks, width, width).transpose(0, 2, 1, 3)
    arrays = {
        "x": x,
        "params": np.concatenate([
            a[n + "Wk"].T, a[n + "Wv"].T, a[n + "Wq"].T, a[n + "Wo"].T, ctx.reshape(batches * keys, width).T,
            np.tile(ctx, (1, width // keys, 1)).reshape(batches * width, width).T,
            a[n + "bq"][:, None], a[n + "bk"][:, None], a[m + "router_w"].T,
            b1.reshape(experts * chunks, width).T, b2.T], axis=1),
        "rows": np.concatenate([a[n + "bo"], a[m + "router_b"], a[n + "bv"]])[None],
        "mask": a["mask_BxS2_ik0"].reshape(1, batches * keys),
        "experts": np.concatenate([w1t, w2t.reshape(experts, width, hidden)], axis=2),
    }
    nc = bacc.Bacc("TRN2", target_bir_lowering=False, num_devices=1)
    feeds, args = {}, []
    for name, value in arrays.items():
        value = np.ascontiguousarray(value)
        feeds[f"in_{name}"] = value
        args.append(nc.dram_tensor(f"in_{name}", value.shape, mybir.dt.from_np(value.dtype),
                                   kind="ExternalInput").ap())
    args.append(nc.dram_tensor("out", _OUT, F32, kind="ExternalOutput").ap())
    xattn_moe_kernel(nc, *args)
    r = run_bass_kernel_spmd(nc, [feeds], core_ids=[0])
    return r.results[0]["out"]
```

```python
from contextlib import ExitStack

import concourse.bass as bass
from concourse import mybir

ALU = mybir.AluOpType
ACT = mybir.ActivationFunctionType
F32 = mybir.dt.float32
F32R = mybir.dt.float32r
I32 = mybir.dt.int32
U32 = mybir.dt.uint32
AX_X = mybir.AxisListType.X

P = 128
HEADS, HD = 16, 8
NEG = -1e30
EPS = 1e-5

C_WK, C_WV, C_WQ, C_WO = 0, P, 2 * P, 3 * P
C_CTX = 4 * P
HALF = 3
PLAIN = 1


def xattn_moe_kernel(nc, x, params, rows, mask, experts, out):
    B, S, D = x.shape
    KEYS = mask.shape[1] // B
    HK = HEADS * KEYS
    T = S // P
    NT = B * T
    NE = experts.shape[0]
    R = NE - 1
    F = experts.shape[2] // 2
    FC = F // P
    HC = HK // P
    HG = P // KEYS
    VC = HG * (HD + 1)
    SCALE = float(HD) ** -0.5
    C_CTX4 = C_CTX + B * KEYS
    C_BQ = C_CTX4 + B * P
    C_BK = C_BQ + 1
    C_WR = C_BQ + 2
    C_B1 = C_WR + R
    C_B2 = C_B1 + NE * FC
    R_BO, R_BR, R_BV = 0, P, P + R
    LAST = NE - 1
    assert params.shape[1] == C_B2 + NE and S == 512 and D == P and HK == 512
    assert B == 2 and HALF % 2 == 1 and (LAST - HALF - 1) % 2 == 0

    combt_dram = nc.dram_tensor("combt_scratch", [R, B, S], F32, kind="Internal").ap()

    def slot(e):
        return e % 2 if e else 2

    with ExitStack() as ctx:
        def sb(name, shape, dt=F32):
            return ctx.enter_context(nc.sbuf_tensor(name, shape, dt))

        def sem(name):
            return ctx.enter_context(nc.semaphore(name))

        par = sb("par", [P, C_B2 + NE])
        rowb = sb("rowb", [P, rows.shape[1]])
        maskb = sb("maskb", [P, B * KEYS], I32)
        ident = sb("ident", [P, P])
        headmask = sb("headmask", [P, HEADS, KEYS])
        groupmask = sb("groupmask", [P, HG])
        iota8 = sb("iota8", [P, R])
        neghalf = sb("neghalf", [P, T])
        gelu_warm = sb("gelu_warm", [P, T])
        xin = sb("xin", [P, B, T, P])
        xb = sb("xb", [P, B, T, P])
        x2 = sb("x2", [P, B, T, P])
        xn = sb("xn", [P, B, T, P])
        stats = sb("stats", [P, T, 6])
        mv = sb("mv", [P, 2, B, T, 2])
        vareps = sb("vareps", [P, 2, B, T])
        rstd = sb("rstd", [P, 2, B, T])
        xt0 = sb("xt0", [P, B, T * P])
        q_hi = sb("q_hi", [P, B, T * P], F32R)
        q_lo = sb("q_lo", [P, B, T * P], F32R)
        k_full = sb("k_full", [P, B * KEYS])
        k_hi = sb("k_hi", [P, B * KEYS])
        k_lo = sb("k_lo", [P, B * KEYS])
        kbd_hi = sb("kbd_hi", [P, B, HEADS, KEYS], F32R)
        kbd_lo = sb("kbd_lo", [P, B, HEADS, KEYS], F32R)
        vb = sb("vb", [P, B, P])
        groupany = sb("groupany", [P, B, HG])
        vaug = sb("vaug", [P, B, HC, HG, HD + 1])
        isvalid = sb("isvalid", [P, B * KEYS])
        anyvalid = sb("anyvalid", [P, B])
        maskrow = sb("maskrow", [1, B, HK], F32R)
        ones_r = sb("ones_r", [1, P], F32R)
        rowmax = sb("rowmax", [P, 2, HEADS])
        probs = sb("probs", [P, T, HK])
        probt = sb("probt", [P, 2, HK])
        rrow = sb("rrow", [P, 2, HEADS])
        on = sb("on", [P, 2, P])
        ont = sb("ont", [P, 2, P])
        xt_hi = sb("xt_hi", [P, B, T * P], F32R)
        xt_lo = sb("xt_lo", [P, B, T * P], F32R)
        wr2 = sb("wr2", [P, 2 * R], F32R)
        loghi = sb("loghi", [P, B, T, R])
        logits = sb("logits", [P, B, T, R])
        top8 = sb("top8", [P, B, T, 8])
        idx8 = sb("idx8", [P, B, T, 8], U32)
        idxf = sb("idxf", [P, B, T, 2])
        gap = sb("gap", [P, B, T])
        w12 = sb("w12", [P, B, T, 2])
        tanhgap = sb("tanhgap", [P, B, T])
        hot = sb("hot", [P, B, T, 2, R])
        hotw = sb("hotw", [P, B, T, 2, R])
        comb = sb("comb", [P, B, T, R])
        combt = sb("combt", [R, B, T * P])
        combb = sb("combb", [P, 2, B, S])
        wst = sb("wst", [P, 3, 2 * F])
        w_hi = [sb(f"w_hi{s}", [P, 2 * F], F32R) for s in range(3)]
        w_lo = [sb(f"w_lo{s}", [P, 2 * F], F32R) for s in range(3)]
        b1cur = sb("b1cur", [P, 2, FC])
        h_full = sb("h_full", [P, FC, B * S])
        h_hi = sb("h_hi", [P, FC, B * S], F32R)
        h_lo = sb("h_lo", [P, FC, B * S], F32R)
        scaled = sb("scaled", [P, B, S])
        acc = sb("acc", [P, B, S])
        lastt = sb("lastt", [P, B, S])
        base = sb("base", [P, B, T, P])
        fin = sb("fin", [P, B, T, P])

        ps = [ctx.enter_context(nc.psum_tensor(f"ps{i}", [P, 1024], F32)) for i in range(4)]

        def bank(i):
            return ps[i // 2][:, 512 * (i % 2):512 * (i % 2) + 512]

        QP = ((0, (0, 1), 5, 1), (0, (2, 3), 0, 2), (1, (0, 1, 2, 3), 0, 1))
        SB = (3, 4)
        TB = 5
        NP = ((0, (0, 1), 0), (0, (2, 3), 1), (1, (0, 1, 2, 3), 4))
        NORMED = (2, 3)
        MB = (6, 7, 2)
        O_, OT_, Y_ = slice(0, HC * VC), slice(256, 384), slice(384, 512)
        DB = (2, 3, 2, 6, 7, 5)
        BB = ((2, 3), (6, 7))

        params_in, biases_in, rows_in, mask_in = (
            sem("params_in"), sem("biases_in"), sem("rows_in"), sem("mask_in"))
        x_in = [sem(f"x_in{b}") for b in range(B)]
        ident_ready, headmask_ready, groupmask_ready, neghalf_ready, iota_ready, ones_ready = (
            sem("ident_ready"), sem("headmask_ready"), sem("groupmask_ready"), sem("neghalf_ready"),
            sem("iota_ready"), sem("ones_ready"))
        xb_ready = sem("xb_ready")
        k_psum, v_psum, k_ready, khi_ready, klo_ready, kbd_ready = (
            sem("k_psum"), sem("v_psum"), sem("k_ready"), sem("khi_ready"), sem("klo_ready"), sem("kbd_ready"))
        valid_ready, any_ready, maskrow_ready = sem("valid_ready"), sem("any_ready"), sem("maskrow_ready")
        groupany_ready, vb_ready, vaug_ready = sem("groupany_ready"), sem("vb_ready"), sem("vaug_ready")
        wr_hi_ready, wr_ready = sem("wr_hi_ready"), sem("wr_ready")
        st_done = [sem(f"ln{k}_stats") for k in range(2)]
        mv_done = [sem(f"ln{k}_meanvar") for k in range(2)]
        ve_done = [sem(f"ln{k}_vareps") for k in range(2)]
        rs_done = [sem(f"ln{k}_rstd") for k in range(2)]
        xn_done = [sem(f"ln{k}_normed") for k in range(2)]
        tr_done = [sem(f"ln{k}_transposed") for k in range(2)]
        xt0_done, q_psum, qhi_done, qlo_done = sem("xt0_done"), sem("q_psum"), sem("qhi_done"), sem("qlo_done")
        xhi_done, xlo_done = sem("xhi_done"), sem("xlo_done")
        scores_done, max_done, shift_done, exp_done = (
            sem("scores_done"), sem("max_done"), sem("shift_done"), sem("exp_done"))
        ptr_done, probt_done, o_done, recip_done, on_done, ot_done, ont_done, y_done, x2_done = (
            sem("ptr_done"), sem("probt_done"), sem("o_done"), sem("recip_done"), sem("on_done"),
            sem("ot_done"), sem("ont_done"), sem("y_done"), sem("x2_done"))
        logit_psum, loghi_ready, logit_ready, top_ready, idx_ready, idxf_ready = (
            sem("logit_psum"), sem("loghi_ready"), sem("logit_ready"), sem("top_ready"), sem("idx_ready"),
            sem("idxf_ready"))
        gap_ready, tanh_ready, w12_ready = sem("gap_ready"), sem("tanh_ready"), sem("w12_ready")
        hot_ready, hotw_ready, comb_ready = sem("hot_ready"), sem("hotw_ready"), sem("comb_ready")
        combt_psum, combt_ready = sem("combt_psum"), sem("combt_ready")
        combt_stored = [sem(f"combt_stored{b}") for b in range(B)]
        half_comb_in = {(e, b): sem(f"half_comb_in{e}_{b}") for e in range(1, HALF) for b in range(B)}
        comb_in = [sem(f"comb_in{s}") for s in range(2)]
        w_in = [sem(f"w_in{s}") for s in range(3)]
        whi_done = [sem(f"w{n + 1}hi_done") for n in range(2)]
        wlo_done = [sem(f"w{n + 1}lo_done") for n in range(2)]
        b1_ready = sem("b1_ready")
        up_done, gelu_done, hhi_done, hlo_done, down_done = (
            sem("up_done"), sem("gelu_done"), sem("hhi_done"), sem("hlo_done"), sem("down_done"))
        acc_init, scaled_done, acc_done = sem("acc_init"), sem("scaled_done"), sem("acc_done")
        last_down, lastt_done, acct_done, base_done = (
            sem("last_down"), sem("lastt_done"), sem("acct_done"), sem("base_done"))
        back_done, fin_done, out_stored = sem("back_done"), sem("fin_done"), sem("out_stored")

        def columns(n, parts=QP):
            return slice(parts[n][1][0] * P, (parts[n][1][-1] + 1) * P)

        HALVE = (slice(0, S // 2), slice(S // 2, S))

        def unit(e):
            return e + HALF

        def hidden_bank(u, f):
            if (u, f) == (0, 2):
                return bank(SB[0])
            return bank(f if u == 2 * HALF - 1 else f % 2)

        def scaled_after(e, b):
            return 2 * (HALF - 1) + 2 * (e - HALF) + b + 1

        HALVES = [(e, b) for b in range(B) for e in range(HALF)]
        SCALED = {(e, b): b * (HALF - 1) + e for e, b in HALVES}

        block = ctx.enter_context(nc.Block())

        @block.sync
        def _(sp):
            sp.dma_start(xin[:, 0], x[0].rearrange("(p t) d -> p t d", t=T)).then_inc(x_in[0], 16)
            sp.dma_start(xin[:, 1], x[1].rearrange("(p t) d -> p t d", t=T)).then_inc(x_in[1], 16)

            def load_weights(e, s):
                sp.dma_start(wst[:, s], experts[e]).then_inc(w_in[s], 16)

            def load_comb(e, s):
                sp.dma_start(combb[:, s], combt_dram[e - 1].partition_broadcast(P)).then_inc(comb_in[s], 16)

            for e in range(HALF):
                load_weights(e, slot(e))
            sp.dma_start(par[:, C_B1:C_B2 + NE], params[:, C_B1:C_B2 + NE]).then_inc(biases_in, 16)
            for b in range(B):
                if b == 1:
                    for e in (HALF, HALF + 1):
                        sp.wait_ge(wlo_done[1], e - 1)
                        if PLAIN > e - 2:
                            sp.wait_ge(down_done, FC * (e - 1))
                        load_weights(e, e % 2)
                sp.wait_ge(combt_ready, b + 1)
                sp.dma_start(combt_dram[:, b], combt[:, b]).then_inc(combt_stored[b], 16)
                sp.wait_ge(combt_stored[b], 16)
                for e in range(1, HALF):
                    sp.dma_start(combb[:, e % 2, b],
                                 combt_dram[e - 1, b:b + 1].partition_broadcast(P)).then_inc(half_comb_in[e, b], 16)
            sp.wait_ge(scaled_done, SCALED[HALF - 2, 1])
            load_comb(HALF, 1)
            with sp.Fori(0, (LAST - HALF - 1) // 2) as i:
                e = i * 2 + HALF
                for j in range(2):
                    sp.wait_ge(wlo_done[1], e + j + 1)
                    load_weights(e + j + 2, 1 - j)
                    sp.wait_ge(scaled_done, scaled_after(e + j - 1, 1))
                    load_comb(e + j + 1, j)
            for b in range(B):
                sp.wait_ge(fin_done, T * (b + 1))
                sp.dma_start(out[b].rearrange("(p t) d -> p t d", t=T), fin[:, b]).then_inc(out_stored, 16)
            sp.wait_ge(out_stored, 16 * B)

        @block.gpsimd
        def _(pool):
            pool.memset(ident[:], 0.0).then_inc(ident_ready, 1)
            pool.memset(neghalf[:], -0.5).then_inc(neghalf_ready, 1)
            pool.memset(headmask[:], 1.0).then_inc(headmask_ready, 1)
            pool.memset(groupmask[:], 1.0).then_inc(groupmask_ready, 1)

            def keep(tile, ready, n, base, pattern, channel):
                pool.wait_ge(ready, n)
                pool.affine_select(out=tile, in_=tile, compare_op=ALU.is_ge, fill=0.0, base=base,
                                   pattern=pattern, channel_multiplier=channel).then_inc(ready, 1)

            pool.wait_ge(ident_ready, 1)
            pool.affine_select(out=ident[:], in_=ident[:], compare_op=ALU.not_equal, fill=1.0, base=0,
                               pattern=[[-1, P]], channel_multiplier=1).then_inc(ident_ready, 1)
            keep(headmask[:], headmask_ready, 1, 0, [[-HD, HEADS], [0, KEYS]], 1)
            keep(headmask[:], headmask_ready, 2, HD - 1, [[HD, HEADS], [0, KEYS]], -1)
            keep(groupmask[:], groupmask_ready, 1, 0, [[-KEYS, HG]], 1)
            keep(groupmask[:], groupmask_ready, 2, KEYS - 1, [[KEYS, HG]], -1)
            pool.iota(iota8[:], pattern=[[1, R]], base=0, channel_multiplier=0,
                      allow_small_or_imprecise_dtypes=True).then_inc(iota_ready, 1)

            def rstd_of(k, b):
                pool.wait_ge(ve_done[k], b + 1)
                pool.tensor_tensor(rstd[:, k, b], vareps[:, k, b], neghalf[:], ALU.pow).then_inc(rs_done[k], 1)

            def block_k(b):
                for part, source in ((kbd_hi, k_hi), (kbd_lo, k_lo)):
                    pool.tensor_tensor(part[:, b], headmask[:],
                                       source[:, b * KEYS:(b + 1) * KEYS].unsqueeze(1)
                                       .broadcast_to([P, HEADS, KEYS]), ALU.mult).then_inc(kbd_ready, 1)

            def mask_row(b):
                pool.tensor_scalar(maskrow[:, b].rearrange("p (h k) -> p h k", h=HEADS),
                                   isvalid[0:1, b * KEYS:(b + 1) * KEYS].unsqueeze(1)
                                   .broadcast_to([1, HEADS, KEYS]),
                                   -NEG, NEG, ALU.mult, ALU.add).then_inc(maskrow_ready, 1)

            def add_bo(b):
                pool.wait_ge(rows_in, 16)
                pool.wait_ge(x_in[b], 16)
                pool.tensor_tensor(xb[:, b], xin[:, b],
                                   rowb[:, R_BO:R_BO + P].unsqueeze(1).broadcast_to([P, T, P]),
                                   ALU.add).then_inc(xb_ready, 1)

            def split_w_lo(e, s, n):
                part = slice(n * F, (n + 1) * F)
                pool.wait_ge(whi_done[n], e + 1)
                pool.tensor_tensor(w_lo[s][:, part], wst[:, s, part], w_hi[s][:, part].bitcast(F32),
                                   ALU.subtract).then_inc(wlo_done[n], 1)

            def accumulate(b, n, before):
                pool.wait_ge(scaled_done, n)
                if before is not None:
                    pool.wait_ge(acc_done, before)
                pool.tensor_tensor(acc[:, b], acc[:, b], scaled[:, b], ALU.add).then_inc(acc_done, 1)

            pool.wait_ge(neghalf_ready, 1)
            rstd_of(0, 0)
            pool.wait_ge(headmask_ready, 3)
            pool.wait_ge(klo_ready, 1)
            block_k(0)
            pool.wait_ge(valid_ready, 1)
            mask_row(0)
            rstd_of(0, 1)
            block_k(1)
            mask_row(1)
            add_bo(0)
            split_w_lo(0, slot(0), 0)
            add_bo(1)
            for e in range(1, HALF):
                split_w_lo(e, slot(e), 0)
            for e in range(HALF - 1):
                split_w_lo(e, slot(e), 1)
            rstd_of(1, 0)
            split_w_lo(HALF - 1, slot(HALF - 1), 1)
            rstd_of(1, 1)
            for e, b in HALVES:
                if (e, b) == (HALF - 2, B - 1):
                    split_w_lo(HALF, 1, 0)
                if e == 1:
                    pool.wait_ge(acc_init, b + 1)
                if e:
                    accumulate(b, SCALED[e, b], SCALED[e, b] - 1 if e > 1 else None)
                if (e, b) == (HALF - 2, B - 1):
                    split_w_lo(HALF, 1, 1)
                    split_w_lo(HALF + 1, 0, 0)
            with pool.Fori(0, (LAST - HALF - 1) // 2) as i:
                e = i * 2 + HALF
                for j in range(2):
                    split_w_lo(e + j + 2, 1 - j, 0)
                    split_w_lo(e + j + 1, j, 1)
                    for b in range(B):
                        accumulate(b, scaled_after(e + j, b), scaled_after(e + j - 1, b))
            split_w_lo(LAST, 0, 1)
            for b in range(B):
                accumulate(b, scaled_after(LAST - 1, b), scaled_after(LAST - 2, b))

        @block.scalar
        def _(act):
            act.dma_start(par[:, 0:C_B1], params[:, 0:C_B1]).then_inc(params_in, 16)
            act.dma_start(rowb[:], rows.partition_broadcast(P)).then_inc(rows_in, 16)
            act.dma_start(maskb[:], mask.partition_broadcast(P)).then_inc(mask_in, 16)

            def copy_xt0(n):
                b, tiles, norm_bank, _ = QP[n]
                act.wait_ge(tr_done[0], n + 1)
                act.activation(xt0[:, b, columns(n)], bank(norm_bank)[:, columns(n)], ACT.Copy).then_inc(xt0_done, 1)

            def q_high(n):
                b, tiles, _, q_bank = QP[n]
                act.wait_ge(q_psum, n + 1)
                act.activation(q_hi[:, b, columns(n)], bank(q_bank)[:, columns(n)], ACT.Identity,
                               bias=par[:, C_BQ:C_BQ + 1]).then_inc(qhi_done, 1)

            def split_first_hi(e, n):
                part = slice(n * F, (n + 1) * F)
                act.wait_ge(w_in[slot(e)], 16)
                act.activation(w_hi[slot(e)][:, part], wst[:, slot(e), part], ACT.Copy).then_inc(whi_done[n], 1)

            def exp(i):
                act.wait_ge(shift_done, i + 1)
                act.activation(probs[:, i % T], probs[:, i % T], ACT.Exp).then_inc(exp_done, 1)

            def copy_probt(i):
                act.wait_ge(ptr_done, i + 1)
                if i >= 2:
                    act.wait_ge(o_done, i - 1)
                act.activation(probt[:, i % 2], bank(TB), ACT.Copy).then_inc(probt_done, 1)

            def copy_ont(i):
                act.wait_ge(ot_done, i + 1)
                if i >= 2:
                    act.wait_ge(y_done, i - 1)
                act.activation(ont[:, i % 2], bank(MB[i % 3])[:, OT_], ACT.Copy).then_inc(ont_done, 1)

            def xt_high(n):
                b, tiles, norm_bank = NP[n]
                act.wait_ge(tr_done[1], n + 1)
                act.activation(xt_hi[:, b, columns(n, NP)], bank(norm_bank)[:, columns(n, NP)],
                               ACT.Copy).then_inc(xhi_done, 1)

            def router_tanh(b):
                act.wait_ge(gap_ready, b + 1)
                act.activation(tanhgap[:, b], gap[:, b], ACT.Tanh, scale=0.5).then_inc(tanh_ready, 1)

            def copy_combt(b):
                act.wait_ge(combt_psum, b + 1)
                act.activation(combt[:, b], bank(TB)[0:R], ACT.Copy).then_inc(combt_ready, 1)

            def gelu_half(u, f):
                e, b = HALVES[u]
                src = hidden_bank(u, f)
                b1 = par[:, C_B1 + e * FC + f:C_B1 + e * FC + f + 1]
                dst = slice(b * S, (b + 1) * S)
                act.wait_ge(up_done, FC * u + f + 1)
                if 0 < u <= PLAIN:
                    act.wait_ge(down_done, FC * (u - 1) + f + 1)
                if u > PLAIN:
                    act.wait_ge(hlo_done, FC * (u - 1 - PLAIN) + f + 1)
                act.activation(h_full[:, f, dst], src, ACT.Gelu_apprx_tanh, bias=b1).then_inc(gelu_done, 1)
                if u >= PLAIN:
                    if u > PLAIN:
                        act.wait_ge(down_done, FC * (u - 1) + f + 1)
                    act.activation(h_hi[:, f, dst], src, ACT.Gelu_apprx_tanh, bias=b1).then_inc(hhi_done, 1)

            def take_b1(e, s):
                act.activation(b1cur[:, s], par[:, bass.ds(C_B1 + e * FC, FC)], ACT.Copy).then_inc(b1_ready, 1)

            def gelu(e, s, f):
                src = ps[f % 2][:]
                b1 = b1cur[:, s, f:f + 1]
                act.wait_ge(b1_ready, e - HALF + 1)
                act.wait_ge(up_done, FC * unit(e) + f + 1)
                act.wait_ge(hlo_done, FC * (unit(e) - 1 - PLAIN) + f + 1)
                act.activation(h_full[:, f], src, ACT.Gelu_apprx_tanh, bias=b1).then_inc(gelu_done, 1)
                act.wait_ge(down_done, FC * (unit(e) - 1) + f + 1)
                act.activation(h_hi[:, f], src, ACT.Gelu_apprx_tanh, bias=b1).then_inc(hhi_done, 1)

            copy_xt0(0)
            copy_xt0(1)
            q_high(0)
            q_high(1)

            def attention_step(s):
                if 3 <= s < NT + 3:
                    copy_ont(s - 3)
                if 1 <= s <= NT:
                    copy_probt(s - 1)
                if s == 2:
                    q_high(2)
                if s < NT:
                    exp(s)
                if s == 1:
                    copy_xt0(2)

            for s in range(T + 4):
                attention_step(s)
                if s < HALF:
                    split_first_hi(s, 0)
                elif s < 2 * HALF:
                    split_first_hi(s - HALF, 1)
            xt_high(0)
            xt_high(1)
            copy_ont(T + 1)
            copy_probt(NT - 1)
            act.wait_ge(neghalf_ready, 1)
            act.activation(gelu_warm[:], neghalf[:], ACT.Gelu_apprx_tanh)
            act.wait_ge(biases_in, 16)
            for u in range(2 * HALF):
                for f in range(FC):
                    if (u, f) == (0, 1):
                        attention_step(T + 5)
                    gelu_half(u, f)
                    if (u, f) == (0, 2):
                        attention_step(T + 6)
                    if (u, f) == (0, 3):
                        router_tanh(0)
                    if (u, f) == (1, 0):
                        copy_combt(0)
                    if (u, f) == (1, 2):
                        xt_high(2)
                    if (u, f) == (2, 2):
                        router_tanh(1)
                    if (u, f) == (3, 2):
                        copy_combt(1)
            take_b1(HALF, 1)
            for f in range(FC):
                gelu(HALF, 1, f)
            take_b1(HALF + 1, 0)
            with act.Fori(0, (LAST - HALF - 1) // 2) as i:
                e = i * 2 + HALF
                for j in range(2):
                    for f in range(FC):
                        gelu(e + j + 1, j, f)
                    take_b1(e + j + 2, 1 - j)
            for f in range(FC):
                gelu(LAST, 0, f)
            for b in range(B):
                act.wait_ge(last_down, b + 1)
                for h in range(2):
                    act.activation(lastt[:, b, HALVE[h]], bank(4 + b)[:, HALVE[h]], ACT.Identity,
                                   bias=par[:, C_B2 + LAST:C_B2 + LAST + 1]).then_inc(lastt_done, 1)

        @block.vector
        def _(dve):
            dve.memset(ones_r[:].bitcast(F32), 1.0).then_inc(ones_ready, 1)

            def tile_stats(k, b, t, src):
                dve.bn_stats(stats[:, t], src[:, b, t]).then_inc(st_done[k], 1)

            def tile_meanvar(k, b, t):
                dve.wait_ge(st_done[k], T * b + t + 1)
                dve.bn_aggr(mv[:, k, b, t], stats[:, t]).then_inc(mv_done[k], 1)

            def var_eps(k, b):
                dve.wait_ge(mv_done[k], T * (b + 1))
                dve.tensor_scalar(vareps[:, k, b], mv[:, k, b, :, 1], EPS, None, ALU.add).then_inc(ve_done[k], 1)

            def norm(k, b, src):
                dve.wait_ge(rs_done[k], b + 1)
                for t in range(T):
                    dve.tensor_scalar(xn[:, b, t], src[:, b, t], mv[:, k, b, t, 0:1], rstd[:, k, b, t:t + 1],
                                      ALU.subtract, ALU.mult).then_inc(xn_done[k], 1)

            def heads(ap):
                return ap.rearrange("p (h k) -> p h k", h=HEADS)

            def q_low(n):
                b, tiles, _, q_bank = QP[n]
                dve.wait_ge(qhi_done, n + 1)
                dve.scalar_tensor_tensor(out=q_lo[:, b, columns(n)], in0=bank(q_bank)[:, columns(n)],
                                         scalar=par[:, C_BQ:C_BQ + 1], in1=q_hi[:, b, columns(n)].bitcast(F32),
                                         op0=ALU.add, op1=ALU.subtract).then_inc(qlo_done, 1)

            def maximum(i):
                dve.wait_ge(scores_done, i + 1)
                dve.tensor_reduce(rowmax[:, i % 2], heads(bank(SB[i % 2])), AX_X, ALU.max).then_inc(max_done, 1)

            def shift(i):
                dve.wait_ge(max_done, i + 1)
                if i >= T:
                    dve.wait_ge(ptr_done, i - T + 1)
                dve.tensor_tensor(heads(probs[:, i % T]), heads(bank(SB[i % 2])),
                                  rowmax[:, i % 2].unsqueeze(2).broadcast_to([P, HEADS, KEYS]),
                                  ALU.subtract).then_inc(shift_done, 1)

            def attention(i):
                return bank(MB[i % 3])[:, O_].rearrange("p (h c) -> p h c", h=HEADS)

            def invert_sums(i):
                dve.wait_ge(o_done, i + 1)
                dve.reciprocal(rrow[:, i % 2], attention(i)[:, :, HD]).then_inc(recip_done, 1)

            def normalise(i):
                dve.wait_ge(recip_done, i + 1)
                if i >= 2:
                    dve.wait_ge(ot_done, i - 1)
                dve.tensor_tensor(on[:, i % 2].rearrange("p (h d) -> p h d", h=HEADS), attention(i)[:, :, 0:HD],
                                  rrow[:, i % 2].unsqueeze(2).broadcast_to([P, HEADS, HD]),
                                  ALU.mult).then_inc(on_done, 1)

            def residual(i):
                dve.wait_ge(y_done, i + 1)
                dve.wait_ge(xb_ready, i // T + 1)
                dve.tensor_tensor(x2[:, i // T, i % T], bank(MB[i % 3])[:, Y_], xb[:, i // T, i % T],
                                  ALU.add).then_inc(x2_done, 1)

            def xt_low(n):
                b, tiles, norm_bank = NP[n]
                dve.wait_ge(xhi_done, n + 1)
                dve.tensor_tensor(xt_lo[:, b, columns(n, NP)], bank(norm_bank)[:, columns(n, NP)],
                                  xt_hi[:, b, columns(n, NP)].bitcast(F32), ALU.subtract).then_inc(xlo_done, 1)

            def split_w_hi(e, s, n):
                part = slice(n * F, (n + 1) * F)
                dve.wait_ge(w_in[s], e * 8 + (8 if s == 1 else 0))
                dve.wait_ge((up_done, down_done)[n], FC * (e + 2))
                dve.tensor_copy(w_hi[s][:, part], wst[:, s, part]).then_inc(whi_done[n], 1)

            def route_top(b):
                dve.wait_ge(logit_psum, b + 1)
                lg = bank(TB)[:, 0:2 * T * R].rearrange("p (t e) -> p t e", t=T)
                dve.tensor_tensor(loghi[:, b], lg[:, :, 0:R],
                                  rowb[:, R_BR:R_BR + R].unsqueeze(1).broadcast_to([P, T, R]),
                                  ALU.add).then_inc(loghi_ready, 1)
                dve.wait_ge(loghi_ready, b + 1)
                dve.tensor_tensor(logits[:, b], lg[:, :, R:2 * R], loghi[:, b], ALU.add).then_inc(logit_ready, 1)
                dve.wait_ge(logit_ready, b + 1)
                for t in range(T):
                    dve.max(top8[:, b, t], logits[:, b, t]).then_inc(top_ready, 1)
                dve.wait_ge(top_ready, T * (b + 1))
                dve.tensor_tensor(gap[:, b], top8[:, b, :, 1], top8[:, b, :, 0], ALU.subtract).then_inc(gap_ready, 1)
                for t in range(T):
                    dve.max_index(idx8[:, b, t], top8[:, b, t], logits[:, b, t]).then_inc(idx_ready, 1)

            def route_weights(b):
                dve.wait_ge(idx_ready, T * (b + 1))
                dve.tensor_copy(idxf[:, b], idx8[:, b, :, 0:2]).then_inc(idxf_ready, 1)
                dve.wait_ge(tanh_ready, b + 1)
                for n, sign in enumerate((-0.5, 0.5)):
                    dve.tensor_scalar(w12[:, b, :, n], tanhgap[:, b], sign, 0.5, ALU.mult,
                                      ALU.add).then_inc(w12_ready, 1)
                dve.wait_ge(idxf_ready, b + 1)
                dve.tensor_tensor(hot[:, b],
                                  iota8[:].unsqueeze(1).unsqueeze(1).broadcast_to([P, T, 2, R]),
                                  idxf[:, b].unsqueeze(3).broadcast_to([P, T, 2, R]),
                                  ALU.is_equal).then_inc(hot_ready, 1)
                dve.wait_ge(w12_ready, 2 * (b + 1))
                dve.wait_ge(hot_ready, b + 1)
                dve.tensor_tensor(hotw[:, b], hot[:, b], w12[:, b].unsqueeze(3).broadcast_to([P, T, 2, R]),
                                  ALU.mult).then_inc(hotw_ready, 1)
                dve.wait_ge(hotw_ready, b + 1)
                dve.tensor_tensor(comb[:, b], hotw[:, b, :, 0], hotw[:, b, :, 1], ALU.add).then_inc(comb_ready, 1)

            dve.wait_ge(x_in[0], 16)
            for t in range(T):
                tile_stats(0, 0, t, xin)
            for t in range(T):
                tile_meanvar(0, 0, t)
            var_eps(0, 0)
            dve.wait_ge(k_psum, 1)
            dve.tensor_scalar(k_full[:], bank(MB[1])[:, 0:B * KEYS], par[:, C_BK:C_BK + 1], SCALE,
                              ALU.add, ALU.mult).then_inc(k_ready, 1)
            dve.wait_ge(k_ready, 1)
            dve.tensor_copy(k_hi[:].bitcast(F32R), k_full[:]).then_inc(khi_ready, 1)
            dve.wait_ge(khi_ready, 1)
            dve.tensor_tensor(k_lo[:], k_full[:], k_hi[:], ALU.subtract).then_inc(klo_ready, 1)
            norm(0, 0, xin)
            dve.wait_ge(x_in[1], 16)
            for t in range(T):
                tile_stats(0, 1, t, xin)
            for t in range(T):
                tile_meanvar(0, 1, t)
            var_eps(0, 1)
            dve.wait_ge(mask_in, 16)
            dve.tensor_scalar(isvalid[:], maskb[:], 0.0, None, ALU.not_equal).then_inc(valid_ready, 1)
            dve.wait_ge(valid_ready, 1)
            dve.tensor_reduce(anyvalid[:], isvalid[:].rearrange("p (b k) -> p b k", b=B), AX_X,
                              ALU.max).then_inc(any_ready, 1)
            q_low(0)
            q_low(1)
            dve.wait_ge(v_psum, 1)
            dve.wait_ge(rows_in, 16)
            dve.tensor_tensor(vb[:], bank(MB[0])[:, 0:B * P].rearrange("p (b d) -> p b d", b=B),
                              rowb[:, R_BV:R_BV + P].unsqueeze(1).broadcast_to([P, B, P]), ALU.add).then_inc(vb_ready, 1)
            dve.wait_ge(groupmask_ready, 3)
            dve.wait_ge(any_ready, 1)
            dve.tensor_tensor(groupany[:], groupmask[:].unsqueeze(1).broadcast_to([P, B, HG]),
                              anyvalid[:].unsqueeze(2).broadcast_to([P, B, HG]), ALU.mult).then_inc(groupany_ready, 1)
            dve.tensor_copy(vaug[:, :, :, :, HD].rearrange("p b c g -> p (b c) g"),
                            groupmask[:].unsqueeze(1).broadcast_to([P, B * HC, HG])).then_inc(vaug_ready, 1)
            dve.wait_ge(vb_ready, 1)
            dve.wait_ge(groupany_ready, 1)
            for b in range(B):
                dve.tensor_tensor(vaug[:, b, :, :, 0:HD],
                                  vb[:, b].rearrange("p (c h d) -> p c h d", c=HC, h=HG),
                                  groupany[:, b].unsqueeze(1).unsqueeze(3).broadcast_to([P, HC, HG, HD]),
                                  ALU.mult).then_inc(vaug_ready, 1)

            def attention_step(s):
                if s >= 4:
                    b, t = divmod(s - 4, T)
                    dve.wait_ge(x2_done, s - 3)
                    tile_stats(1, b, t, x2)
                    if t == T - 1:
                        tile_meanvar(1, b, t)
                        var_eps(1, b)
                if s < NT:
                    maximum(s)
                if 2 <= s < NT + 2:
                    invert_sums(s - 2)
                if s < NT:
                    shift(s)
                if s == 2:
                    q_low(2)
                if s >= 4 and t < T - 1:
                    tile_meanvar(1, b, t)
                if s == T + 3:
                    norm(1, 0, x2)
                if 2 <= s < NT + 2:
                    normalise(s - 2)
                if 3 <= s < NT + 3:
                    residual(s - 3)

            for s in range(T + 5):
                attention_step(s)
                if s == 0:
                    norm(0, 1, xin)
                if s == T + 3:
                    xt_low(0)
                    xt_low(1)
                if s == 1:
                    dve.tensor_copy(wr2[:, 0:R], par[:, C_WR:C_WR + R]).then_inc(wr_hi_ready, 1)
                    dve.wait_ge(wr_hi_ready, 1)
                    dve.tensor_tensor(wr2[:, R:2 * R], par[:, C_WR:C_WR + R], wr2[:, 0:R].bitcast(F32),
                                      ALU.subtract).then_inc(wr_ready, 1)
            attention_step(T + 5)
            route_top(0)
            attention_step(T + 6)
            attention_step(T + 7)
            route_weights(0)
            norm(1, 1, x2)
            dve.wait_ge(biases_in, 16)

            def start_sum(b, u):
                dve.wait_ge(down_done, FC * (u + 1))
                dve.tensor_scalar(acc[:, b], bank(DB[u]), par[:, C_B2:C_B2 + 1], None,
                                  ALU.add).then_inc(acc_init, 1)

            def weigh_half(u):
                e, b = HALVES[u]
                dve.wait_ge(down_done, FC * (u + 1))
                dve.wait_ge(half_comb_in[e, b], 16)
                if e > 1:
                    dve.wait_ge(acc_done, SCALED[e, b] - 1)
                dve.scalar_tensor_tensor(out=scaled[:, b], in0=bank(DB[u]), scalar=par[:, C_B2 + e:C_B2 + e + 1],
                                         in1=combb[:, e % 2, b], op0=ALU.add, op1=ALU.mult).then_inc(scaled_done, 1)

            def h_low_half(u, f):
                dst = slice(HALVES[u][1] * S, (HALVES[u][1] + 1) * S)
                dve.wait_ge(gelu_done, FC * u + f + 1)
                dve.wait_ge(hhi_done, FC * (u - PLAIN) + f + 1)
                dve.tensor_tensor(h_lo[:, f, dst], h_full[:, f, dst], h_hi[:, f, dst].bitcast(F32),
                                  ALU.subtract).then_inc(hlo_done, 1)

            for u in range(PLAIN, 2 * HALF):
                for f in range(FC):
                    if f == FC - 1 and u > 0:
                        if HALVES[u - 1][0]:
                            weigh_half(u - 1)
                        else:
                            start_sum(HALVES[u - 1][1], u - 1)
                    h_low_half(u, f)
                    if (u, f) == (1, 2):
                        xt_low(2)
                    if (u, f) == (2, 1):
                        route_top(1)
                    if (u, f) == (2, 3):
                        route_weights(1)
                    if (u, f) == (2 * HALF - 1, 0):
                        split_w_hi(HALF, 1, 0)

            def h_low(e, f):
                dve.wait_ge(gelu_done, FC * unit(e) + f + 1)
                dve.wait_ge(hhi_done, FC * (unit(e) - PLAIN) + f + 1)
                dve.tensor_tensor(h_lo[:, f], h_full[:, f], h_hi[:, f].bitcast(F32),
                                  ALU.subtract).then_inc(hlo_done, 1)

            def weigh(e, s):
                b2 = par[:, bass.ds(C_B2 + e, 1)]
                dve.wait_ge(down_done, FC * (unit(e) + 1))
                dve.wait_ge(comb_in[s], e * 8 - (8 if s == 1 else 16))
                for b in range(B):
                    dve.wait_ge(acc_done, scaled_after(e - 1, b))
                    dve.scalar_tensor_tensor(out=scaled[:, b], in0=ps[2 + s][:, b * S:(b + 1) * S], scalar=b2,
                                             in1=combb[:, s, b], op0=ALU.add, op1=ALU.mult).then_inc(scaled_done, 1)

            split_w_hi(HALF, 1, 1)
            h_low(HALF, 0)
            split_w_hi(HALF + 1, 0, 0)
            for f in range(1, FC):
                h_low(HALF, f)
            weigh_half(2 * HALF - 1)
            with dve.Fori(0, (LAST - HALF - 1) // 2) as i:
                e = i * 2 + HALF
                for j in range(2):
                    h_low(e + j + 1, 0)
                    split_w_hi(e + j + 2, 1 - j, 0)
                    split_w_hi(e + j + 1, j, 1)
                    for f in range(1, FC):
                        h_low(e + j + 1, f)
                    weigh(e + j, 1 - j)
            h_low(LAST, 0)
            split_w_hi(LAST, 0, 1)
            for f in range(1, FC - 1):
                h_low(LAST, f)
            weigh(LAST - 1, 1)
            h_low(LAST, FC - 1)
            for b in range(B):
                dve.wait_ge(acct_done, b + 1)
                dve.tensor_tensor(base[:, b].rearrange("p t d -> p (t d)"), bank(b),
                                  x2[:, b].rearrange("p t d -> p (t d)"), ALU.add).then_inc(base_done, 1)
            for b in range(B):
                dve.wait_ge(base_done, b + 1)
                for t in range(T):
                    dve.wait_ge(back_done, 2 * b + t // 2 + 1)
                    dve.scalar_tensor_tensor(out=fin[:, b, t], in0=bank(BB[b][t // 2])[:, t * P:(t + 1) * P],
                                             scalar=comb[:, b, t, LAST - 1:LAST], in1=base[:, b, t],
                                             op0=ALU.mult, op1=ALU.add).then_inc(fin_done, 1)

        @block.tensor
        def _(pe):
            def keep_clock(n, bank_no):
                for _ in range(n):
                    pe.transpose(bank(bank_no)[:, 0:P], ident[:], ident[:])

            def transpose_first(n):
                b, tiles, norm_bank, _ = QP[n]
                if n == 2:
                    pe.wait_ge(xt0_done, 2)
                for t in tiles:
                    pe.wait_ge(xn_done[0], T * b + t + 1)
                    mm = pe.transpose(bank(norm_bank)[:, t * P:(t + 1) * P], xn[:, b, t], ident[:])
                mm.then_inc(tr_done[0], 1)

            def project_q(n):
                b, tiles, _, q_bank = QP[n]
                pe.wait_ge(xt0_done, n + 1)
                if n == 2:
                    pe.wait_ge(qlo_done, 1)
                pe.matmul(bank(q_bank)[:, columns(n)], par[:, C_WQ:C_WQ + P], xt0[:, b, columns(n)],
                          start=True, stop=True).then_inc(q_psum, 1)

            def transpose_second(n):
                b, tiles, norm_bank = NP[n]
                for t in tiles:
                    pe.wait_ge(xn_done[1], T * b + t + 1)
                    mm = pe.transpose(bank(norm_bank)[:, t * P:(t + 1) * P], xn[:, b, t], ident[:])
                mm.then_inc(tr_done[1], 1)

            def scores(i):
                b, t = divmod(i, T)
                for n, (part_b, tiles, _, _) in enumerate(QP):
                    if (b, t) == (part_b, tiles[0]):
                        pe.wait_ge(qlo_done, n + 1)
                if t == 0:
                    pe.wait_ge(kbd_ready, 2 * (b + 1))
                    pe.wait_ge(maskrow_ready, b + 1)
                if i >= 2:
                    pe.wait_ge(shift_done, i - 1)
                qh, ql = (a[:, b, t * P:(t + 1) * P] for a in (q_hi, q_lo))
                kh, kl = (a[:, b].rearrange("p h k -> p (h k)") for a in (kbd_hi, kbd_lo))
                o = bank(SB[i % 2])
                pe.matmul(o, ones_r[:], maskrow[:, b], start=True, stop=False)
                pe.matmul(o, qh, kl, start=False, stop=False)
                pe.matmul(o, ql, kh, start=False, stop=False)
                pe.matmul(o, qh, kh, start=False, stop=True).then_inc(scores_done, 1)

            def transpose_probs(i):
                pe.wait_ge(exp_done, i + 1)
                if i >= 1:
                    pe.wait_ge(probt_done, i)
                for c in range(HC):
                    mm = pe.transpose(bank(TB)[:, c * P:(c + 1) * P], probs[:, i % T, c * P:(c + 1) * P], ident[:])
                mm.then_inc(ptr_done, 1)

            def attend(i):
                pe.wait_ge(probt_done, i + 1)
                if i == 0:
                    pe.wait_ge(vaug_ready, 1 + B)
                if i == 2:
                    pe.wait_ge(qlo_done, 2)
                if i > 2:
                    pe.wait_ge(x2_done, i - 2)
                for c in range(HC):
                    mm = pe.matmul(bank(MB[i % 3])[:, c * VC:(c + 1) * VC], probt[:, i % 2, c * P:(c + 1) * P],
                                   vaug[:, i // T, c].rearrange("p h c -> p (h c)"), start=True, stop=True)
                mm.then_inc(o_done, 1)

            def transpose_on(i):
                pe.wait_ge(on_done, i + 1)
                pe.transpose(bank(MB[i % 3])[:, OT_], on[:, i % 2], ident[:]).then_inc(ot_done, 1)

            def project_out(i):
                pe.wait_ge(ont_done, i + 1)
                pe.matmul(bank(MB[i % 3])[:, Y_], ont[:, i % 2], par[:, C_WO:C_WO + P],
                          start=True, stop=True).then_inc(y_done, 1)

            def router(b):
                pe.wait_ge(xlo_done, NORMED[b])
                pe.wait_ge(probt_done, NT)
                for t in range(T):
                    o = bank(TB)[:, t * 2 * R:(t + 1) * 2 * R]
                    pe.matmul(o, xt_lo[:, b, t * P:(t + 1) * P], wr2[:], start=True, stop=False)
                    mm = pe.matmul(o, xt_hi[:, b, t * P:(t + 1) * P], wr2[:], start=False, stop=True)
                mm.then_inc(logit_psum, 1)

            def transpose_comb(b):
                pe.wait_ge(comb_ready, b + 1)
                for t in range(T):
                    mm = pe.transpose(bank(TB)[0:R, t * P:(t + 1) * P], comb[:, b, t], ident[:])
                mm.then_inc(combt_psum, 1)

            def up_half(u, f):
                e, b = HALVES[u]
                if f == 0:
                    pe.wait_ge(wlo_done[0], e + 1)
                    pe.wait_ge(xlo_done, NORMED[b])
                n = FC * u + f - 1
                if (u, f) == (0, 2):
                    pe.wait_ge(shift_done, NT - 1)
                elif n > 0 and n <= FC * PLAIN:
                    pe.wait_ge(gelu_done, n)
                elif n > 0:
                    pe.wait_ge(hhi_done, n - FC * PLAIN)
                if u == 2 * HALF - 1 and f == 2:
                    pe.wait_ge(scaled_done, SCALED[HALVES[2]])
                wh, wl = (w[slot(e)][:, f * P:(f + 1) * P] for w in (w_hi, w_lo))
                o = hidden_bank(u, f)
                pe.matmul(o, wl, xt_hi[:, b], start=True, stop=False)
                pe.matmul(o, wh, xt_lo[:, b], start=False, stop=False)
                pe.matmul(o, wh, xt_hi[:, b], start=False, stop=True).then_inc(up_done, 1)

            def down_half(u, f):
                e, b = HALVES[u]
                o = bank(DB[u])
                if f == 0:
                    if u == 0:
                        pe.wait_ge(x2_done, NT - 2)
                    if u == 1:
                        pe.wait_ge(shift_done, NT)
                    if u == 2:
                        pe.wait_ge(acc_init, 1)
                    if u == 3:
                        pe.wait_ge(x2_done, NT - 1)
                    if u == 4:
                        pe.wait_ge(x2_done, NT)
                    if u == 5:
                        pe.wait_ge(combt_ready, B)
                w2 = slice(F + f * P, F + (f + 1) * P)
                dst = slice(b * S, (b + 1) * S)
                first, last = f == 0, f == FC - 1
                if u < PLAIN:
                    pe.wait_ge(gelu_done, FC * u + f + 1)
                    pe.matmul(o, wst[:, slot(e), w2], h_full[:, f, dst], start=first,
                              stop=last).then_inc(down_done, 1)
                else:
                    pe.wait_ge(wlo_done[1], e + 1)
                    pe.wait_ge(hlo_done, FC * (u - PLAIN) + f + 1)
                    pe.matmul(o, w_lo[slot(e)][:, w2], h_hi[:, f, dst], start=first, stop=False)
                    pe.matmul(o, w_hi[slot(e)][:, w2], h_lo[:, f, dst], start=False, stop=False)
                    pe.matmul(o, w_hi[slot(e)][:, w2], h_hi[:, f, dst], start=False,
                              stop=last).then_inc(down_done, 1)

            def up(e, s, f):
                if f == 0:
                    pe.wait_ge(wlo_done[0], e + 1)
                pe.wait_ge(hhi_done, FC * (unit(e) - PLAIN) + (f - 1))
                wh, wl = (w[s][:, f * P:(f + 1) * P] for w in (w_hi, w_lo))
                for b in range(B):
                    o = ps[f % 2][:, b * S:(b + 1) * S]
                    pe.matmul(o, wl, xt_hi[:, b], start=True, stop=False)
                    pe.matmul(o, wh, xt_lo[:, b], start=False, stop=False)
                    mm = pe.matmul(o, wh, xt_hi[:, b], start=False, stop=True)
                mm.then_inc(up_done, 1)

            def down(e, s, f):
                if f == 0:
                    pe.wait_ge(scaled_done, scaled_after(e - 2, 1))
                    pe.wait_ge(wlo_done[1], e + 1)
                pe.wait_ge(hlo_done, FC * (unit(e) - PLAIN) + f + 1)
                wh, wl = (w[s][:, F + f * P:F + (f + 1) * P] for w in (w_hi, w_lo))
                for b in range(B):
                    o = ps[2 + s][:, b * S:(b + 1) * S]
                    hh, hl = (h[:, f, b * S:(b + 1) * S] for h in (h_hi, h_lo))
                    pe.matmul(o, wl, hh, start=(f == 0), stop=False)
                    pe.matmul(o, wh, hl, start=False, stop=False)
                    mm = pe.matmul(o, wh, hh, start=False, stop=(f == FC - 1))
                mm.then_inc(down_done, 1)

            pe.wait_ge(ident_ready, 2)
            keep_clock(13, SB[0])
            pe.wait_ge(params_in, 16)
            pe.matmul(bank(MB[1])[:, 0:B * KEYS], par[:, C_WK:C_WK + P],
                      par[:, C_CTX:C_CTX + B * KEYS], start=True, stop=True).then_inc(k_psum, 1)
            for b in range(B):
                mm = pe.matmul(bank(MB[0])[:, b * P:(b + 1) * P], par[:, C_CTX4 + b * P:C_CTX4 + (b + 1) * P],
                               par[:, C_WV:C_WV + P], start=True, stop=True)
            mm.then_inc(v_psum, 1)
            keep_clock(2, SB[0])
            transpose_first(0)
            transpose_first(1)
            keep_clock(2, SB[0])
            project_q(0)
            project_q(1)
            keep_clock(3, SB[0])
            pe.wait_ge(ones_ready, 1)
            scores(0)

            def attention_step(s):
                if s + 1 < NT:
                    scores(s + 1)
                if 3 <= s < NT + 3:
                    project_out(s - 3)
                if 1 <= s <= NT:
                    attend(s - 1)
                if s == T + 3:
                    transpose_second(0)
                    transpose_second(1)
                if 2 <= s < NT + 2:
                    transpose_on(s - 2)
                if s == 0:
                    keep_clock(10, TB)
                if s < NT:
                    transpose_probs(s)

            for s in range(T + 4):
                attention_step(s)
                if s == 0:
                    transpose_first(2)
                if s == 1:
                    project_q(2)
            project_out(T + 1)
            up_half(0, 0)
            attend(NT - 1)
            transpose_on(T + 2)
            up_half(0, 1)
            up_half(0, 2)
            attention_step(T + 5)
            up_half(0, 3)
            pe.wait_ge(wr_ready, 1)
            router(0)
            attention_step(T + 6)
            for u in range(1, 2 * HALF):
                for f in range(FC):
                    if (u, f) == (1, 3):
                        pe.wait_ge(shift_done, NT)
                        transpose_second(2)
                    if (u, f) == (2, 1):
                        pe.wait_ge(combt_ready, 1)
                        router(1)
                    if (u, f) == (3, 3):
                        transpose_comb(1)
                    if u == 1:
                        down_half(u - 1, f)
                    if (u, f) == (1, 2):
                        transpose_comb(0)
                    up_half(u, f)
                    if u > 1:
                        down_half(u - 1, f)
            for f in range(FC):
                up(HALF, 1, f)
                down_half(2 * HALF - 1, f)
            pe.wait_ge(scaled_done, SCALED[HALF - 2, 1])
            with pe.Fori(0, (LAST - HALF - 1) // 2) as i:
                e = i * 2 + HALF
                for j in range(2):
                    for f in range(FC):
                        up(e + j + 1, j, f)
                        down(e + j, 1 - j, f)
            for f in range(FC):
                up(LAST, 0, f)
                down(LAST - 1, 1, f)

            def down_last(f, b):
                pe.wait_ge(hlo_done, FC * (unit(LAST) - PLAIN) + f + 1)
                w2 = slice(F + f * P, F + (f + 1) * P)
                hh, hl = (h[:, f, b * S:(b + 1) * S] for h in (h_hi, h_lo))
                pe.matmul(bank(4 + b), w_lo[0][:, w2], hh, start=(f == 0), stop=False)
                pe.matmul(bank(4 + b), w_hi[0][:, w2], hl, start=False, stop=False)
                return pe.matmul(bank(4 + b), w_hi[0][:, w2], hh, start=False, stop=(f == FC - 1))

            def transpose_acc(b):
                pe.wait_ge(hhi_done, FC * (unit(LAST) + 1 - PLAIN))
                pe.wait_ge(acc_done, scaled_after(LAST - 1, b))
                for t in range(T):
                    mm = pe.transpose(bank(b)[:, t * P:(t + 1) * P], acc[:, b, t * P:(t + 1) * P], ident[:])
                mm.then_inc(acct_done, 1)

            def transpose_last(b):
                for t in range(T):
                    pe.wait_ge(lastt_done, 2 * b + t // 2 + 1)
                    mm = pe.transpose(bank(BB[b][t // 2])[:, t * P:(t + 1) * P],
                                      lastt[:, b, t * P:(t + 1) * P], ident[:])
                    if t % 2:
                        mm.then_inc(back_done, 1)

            pe.wait_ge(scaled_done, scaled_after(LAST - 2, 1))
            pe.wait_ge(wlo_done[1], LAST + 1)
            for f in range(FC - 1):
                down_last(f, 0)
            down_last(0, 1)
            down_last(FC - 1, 0).then_inc(last_down, 1)
            down_last(1, 1)
            transpose_acc(0)
            transpose_acc(1)
            for f in range(2, FC - 1):
                down_last(f, 1)
            pe.wait_ge(scaled_done, scaled_after(LAST - 1, 1))
            transpose_last(0)
            down_last(FC - 1, 1).then_inc(last_down, 1)
            transpose_last(1)


_OUT = (2, 512, 128)


def kernel(**inputs):
    import numpy as np
    import concourse.bacc as bacc
    from concourse.bass_utils import run_bass_kernel_spmd

    a = {k: np.asarray(v) for k, v in inputs.items()}
    n = "L0_xattn_"
    m = "L0_ffn_"
    x, ctx = a["x"], a["ctx_1024"]
    batches, keys, width = ctx.shape
    w1 = np.concatenate([a[m + "shared_w1"][None], a[m + "spec_w1"]])
    w2 = np.concatenate([a[m + "shared_w2"][None], a[m + "spec_w2"]])
    b1 = np.concatenate([a[m + "shared_b1"][None], a[m + "spec_b1"]])
    b2 = np.concatenate([a[m + "shared_b2"][None], a[m + "spec_b2"]])
    experts, hidden, _ = w1.shape
    chunks = hidden // width
    w1t = w1.transpose(0, 2, 1)
    w2t = w2.transpose(0, 2, 1).reshape(experts, chunks, width, width).transpose(0, 2, 1, 3)
    arrays = {
        "x": x,
        "params": np.concatenate([
            a[n + "Wk"].T, a[n + "Wv"].T, a[n + "Wq"].T, a[n + "Wo"].T, ctx.reshape(batches * keys, width).T,
            np.tile(ctx, (1, width // keys, 1)).reshape(batches * width, width).T,
            a[n + "bq"][:, None], a[n + "bk"][:, None], a[m + "router_w"].T,
            b1.reshape(experts * chunks, width).T, b2.T], axis=1),
        "rows": np.concatenate([a[n + "bo"], a[m + "router_b"], a[n + "bv"]])[None],
        "mask": a["mask_BxS2_ik0"].reshape(1, batches * keys),
        "experts": np.concatenate([w1t, w2t.reshape(experts, width, hidden)], axis=2),
    }
    nc = bacc.Bacc("TRN2", target_bir_lowering=False, num_devices=1)
    feeds, args = {}, []
    for name, value in arrays.items():
        value = np.ascontiguousarray(value)
        feeds[f"in_{name}"] = value
        args.append(nc.dram_tensor(f"in_{name}", value.shape, mybir.dt.from_np(value.dtype),
                                   kind="ExternalInput").ap())
    args.append(nc.dram_tensor("out", _OUT, F32, kind="ExternalOutput").ap())
    xattn_moe_kernel(nc, *args)
    r = run_bass_kernel_spmd(nc, [feeds], core_ids=[0])
    return r.results[0]["out"]
```
